# Optimizing a Trainium2 kernel written in Bass

```python
import numpy as np
import jax
import jax.numpy as jnp

def _softmax(x, axis=-1):
    return jax.nn.softmax(x, axis=axis)

def _gelu(x):
    return jax.nn.gelu(x, approximate=True)

def _silu(x):
    return jax.nn.silu(x)

def _sigmoid(x):
    return jax.nn.sigmoid(x)

def _layernorm(x, axis=-1, eps=1e-05):
    m = jnp.mean(x, axis=axis, keepdims=True)
    v = jnp.var(x, axis=axis, keepdims=True)
    return (x - m) / jnp.sqrt(v + eps)

def _scatter_add(tgt, idx, src, axis=0):
    return tgt.at[idx].add(src)

def _segment_sum(src, seg, n):
    return jax.ops.segment_sum(src, seg, n)
kernel_name = 'mk_macaron_d1_jaxref_r8_f735e7'

def setup_inputs(seed: int=0):
    np.random.seed(seed)
    _w = jnp.asarray

    def _L0_attn_setup():
        import jax, jax.numpy as jnp
        import numpy as np
        D_MODEL = 128
        N_HEADS = 16
        D_HEAD = D_MODEL // N_HEADS
        EPS = 1e-06
        B, N = (1, 256)

        def _phi(x):
            return jax.nn.elu(x) + 1.0

        def _split_heads(y, b, n):
            return y.reshape(b, n, N_HEADS, D_HEAD).transpose(0, 2, 1, 3)
        key = jax.random.key(seed)
        ks = jax.random.split(key, 10)
        s = 1.0 / np.sqrt(D_MODEL)
        return {'x': jax.random.normal(ks[0], (B, N, D_MODEL), dtype=jnp.float32), 'mask': jnp.tril(jnp.ones((N, N), dtype=bool)), 'Wq': jax.random.normal(ks[1], (D_MODEL, D_MODEL), dtype=jnp.float32) * s, 'bq': jax.random.normal(ks[2], (D_MODEL,), dtype=jnp.float32) * s, 'Wk': jax.random.normal(ks[3], (D_MODEL, D_MODEL), dtype=jnp.float32) * s, 'bk': jax.random.normal(ks[4], (D_MODEL,), dtype=jnp.float32) * s, 'Wv': jax.random.normal(ks[5], (D_MODEL, D_MODEL), dtype=jnp.float32) * s, 'bv': jax.random.normal(ks[6], (D_MODEL,), dtype=jnp.float32) * s, 'Wo': jax.random.normal(ks[7], (D_MODEL, D_MODEL), dtype=jnp.float32) * s, 'bo': jax.random.normal(ks[8], (D_MODEL,), dtype=jnp.float32) * s}
    _L0_attn_in = _L0_attn_setup()

    def _L0_ffn_setup():
        import jax, jax.numpy as jnp
        import numpy as np
        NUM_EXPERTS = 8
        TOP_K = 2
        B, S, D, DF = (4, 256, 128, 512)
        key = jax.random.key(seed)
        ks = jax.random.split(key, 5)
        scale_in = 1.0 / np.sqrt(D)
        scale_ff = 1.0 / np.sqrt(DF)
        return {'x': jax.random.normal(ks[0], (B, S, D), dtype=jnp.float32), 'Wg': jax.random.normal(ks[1], (D, NUM_EXPERTS), dtype=jnp.float32) * scale_in, 'W1': jax.random.normal(ks[2], (NUM_EXPERTS, D, DF), dtype=jnp.float32) * scale_in, 'b1': jnp.zeros((NUM_EXPERTS, DF), dtype=jnp.float32), 'W2': jax.random.normal(ks[3], (NUM_EXPERTS, DF, D), dtype=jnp.float32) * scale_ff, 'b2': jnp.zeros((NUM_EXPERTS, D), dtype=jnp.float32)}
    _L0_ffn_in = _L0_ffn_setup()
    _d = {'L0_attn_x': _L0_attn_in['x'], 'L0_attn_mask': _L0_attn_in['mask'], 'L0_attn_Wq': _L0_attn_in['Wq'], 'L0_attn_bq': _L0_attn_in['bq'], 'L0_attn_Wk': _L0_attn_in['Wk'], 'L0_attn_bk': _L0_attn_in['bk'], 'L0_attn_Wv': _L0_attn_in['Wv'], 'L0_attn_bv': _L0_attn_in['bv'], 'L0_attn_Wo': _L0_attn_in['Wo'], 'L0_attn_bo': _L0_attn_in['bo'], 'L0_ffn_Wg': _L0_ffn_in['Wg'], 'L0_ffn_W1': _L0_ffn_in['W1'], 'L0_ffn_b1': _L0_ffn_in['b1'], 'L0_ffn_W2': _L0_ffn_in['W2'], 'L0_ffn_b2': _L0_ffn_in['b2']}
    _x0 = _d['L0_attn_x']
    _d['L0_attn_x'] = jax.random.normal(jax.random.fold_in(jax.random.key(seed), 1), (1, 2048, 128), dtype=_x0.dtype)
    del _x0
    return _d

def reference(L0_attn_x, L0_attn_mask, L0_attn_Wq, L0_attn_bq, L0_attn_Wk, L0_attn_bk, L0_attn_Wv, L0_attn_bv, L0_attn_Wo, L0_attn_bo, L0_ffn_Wg, L0_ffn_W1, L0_ffn_b1, L0_ffn_W2, L0_ffn_b2):

    def _L0_attn_ref(x, mask, Wq, bq, Wk, bk, Wv, bv, Wo, bo):
        import jax, jax.numpy as jnp
        import numpy as np
        D_MODEL = 128
        N_HEADS = 16
        D_HEAD = D_MODEL // N_HEADS
        EPS = 1e-06
        B, N = (1, 256)

        def _phi(x):
            return jax.nn.elu(x) + 1.0

        def _split_heads(y, b, n):
            return y.reshape(b, n, N_HEADS, D_HEAD).transpose(0, 2, 1, 3)
        b, n, _ = x.shape
        q = _phi(_split_heads(x @ Wq.T + bq, b, n))
        k = _phi(_split_heads(x @ Wk.T + bk, b, n))
        v = _split_heads(x @ Wv.T + bv, b, n)
        kv = jnp.einsum('bhnd,bhne->bhnde', k, v)
        kv_prefix = jnp.cumsum(kv, axis=2)
        k_prefix = jnp.cumsum(k, axis=2)
        numer = jnp.einsum('bhnd,bhnde->bhne', q, kv_prefix)
        denom = jnp.einsum('bhnd,bhnd->bhn', q, k_prefix)[..., None]
        out_heads = numer / (denom + EPS)
        merged = out_heads.transpose(0, 2, 1, 3).reshape(b, n, D_MODEL)
        return merged @ Wo.T + bo

    def _L0_ffn_ref(x, Wg, W1, b1, W2, b2):
        import jax, jax.numpy as jnp
        import numpy as np
        NUM_EXPERTS = 8
        TOP_K = 2
        B, S, D, DF = (4, 256, 128, 512)
        gate_logits = jnp.einsum('bsd,de->bse', x, Wg)
        top_w, top_i = jax.lax.top_k(gate_logits, TOP_K)
        top_w = jax.nn.softmax(top_w.astype(jnp.float32), axis=-1).astype(x.dtype)
        onehot = jax.nn.one_hot(top_i, NUM_EXPERTS, dtype=x.dtype)
        w_per_expert = jnp.einsum('bske,bsk->bse', onehot, top_w)
        results = jnp.zeros_like(x)
        for i in range(NUM_EXPERTS):
            h = jax.nn.gelu(jnp.einsum('bsd,df->bsf', x, W1[i]) + b1[i])
            out_i = jnp.einsum('bsf,fd->bsd', h, W2[i]) + b2[i]
            results = results + w_per_expert[..., i:i + 1] * out_i
        return results
    x = L0_attn_x
    x = x + 0.5 * _L0_ffn_ref(_layernorm(x, axis=-1), L0_ffn_Wg, L0_ffn_W1, L0_ffn_b1, L0_ffn_W2, L0_ffn_b2)
    x = x + _L0_attn_ref(_layernorm(x, axis=-1), L0_attn_mask, L0_attn_Wq, L0_attn_bq, L0_attn_Wk, L0_attn_bk, L0_attn_Wv, L0_attn_bv, L0_attn_Wo, L0_attn_bo)
    x = x + 0.5 * _L0_ffn_ref(_layernorm(x, axis=-1), L0_ffn_Wg, L0_ffn_W1, L0_ffn_b1, L0_ffn_W2, L0_ffn_b2)
    return x

_drawn_inputs = setup_inputs


def setup_inputs(seed=0):
    import zlib

    import numpy as np

    out = dict(_drawn_inputs(seed))
    spreads = {'L0_ffn_b1': (0.0, 0.1), 'L0_ffn_b2': (0.0, 0.1)}
    factors = {'L0_attn_bq': 22.089, 'L0_attn_bk': 26.072, 'L0_attn_Wq': 3.116}
    for name, (base, spread) in spreads.items():
        noise = np.random.default_rng([zlib.crc32(name.encode()), seed]).standard_normal(out[name].shape)
        drawn = base * np.exp(spread * noise) if base else spread * noise
        out[name] = jnp.asarray(drawn.astype(out[name].dtype))
    for name, factor in factors.items():
        out[name] = (out[name] * factor).astype(out[name].dtype)
    return out
```

```python
from contextlib import ExitStack

import concourse.bass as bass
from concourse import mybir

F32 = mybir.dt.float32
BF16 = mybir.dt.bfloat16
I32 = mybir.dt.int32
U32 = mybir.dt.uint32
ALU = mybir.AluOpType
ACT = mybir.ActivationFunctionType
AX = mybir.AxisListType

P = 128
RING = 3


def at_least(eng, sem, value):
    if isinstance(value, int) and value <= 0:
        return
    eng.wait_ge(sem, value)


def macaron_kernel(nc, x_d, Wq, bq, Wk, bk, Wv, bv, Wo, bo, Wg, W1, b1, W2, b2, out_d):
    T, D = x_d.shape[1], x_d.shape[2]
    E, _, DF = W1.shape
    H, DH = 16, D // 16
    NT = T // P
    FC = DF // P
    TOPK = 2
    NS = (TOPK * T + E * (P - 1)) // P
    QD = 3 * D
    VE = DH + 1
    PAD = 2 * TOPK * T
    LN_EPS, ATT_EPS = 1e-5, 1e-6
    CH = 4
    NC = NT // CH
    assert D == P and NS % RING == 0 and T & (T - 1) == 0

    with ExitStack() as ctx:
        def sb(name, shape, dt=F32):
            return ctx.enter_context(nc.sbuf_tensor(name, shape, dt))

        def sem(name):
            return ctx.enter_context(nc.semaphore(name))

        banks = ctx.enter_context(nc.psum_tensor("banks", [P, 8, 512], F32))

        ident = sb("ident", [P, P])
        tri = sb("tri", [P, P])
        strict_bf = sb("strict_bf", [P, P], BF16)
        ones_bf = sb("ones_bf", [P, P], BF16)
        ones_row = sb("ones_row", [1, P])
        before = sb("before", [P, E, E])
        head_mask = sb("head_mask", [P, H, VE])
        slot_no = sb("slot_no", [P, NS])
        lane_no = sb("lane_no", [P, P])
        full_tiles = sb("full_tiles", [P, NT])
        pair_no = sb("pair_no", [P, TOPK * NT])
        own_lane = sb("own_lane", [P, 1])

        w1 = sb("w1", [P, E * DF])
        w2 = sb("w2", [P, E * DF])
        b1_all = sb("b1_all", [P, E * DF])
        b2_all = sb("b2_all", [P, E * D])
        wg = sb("wg", [P, E])
        w_raw = sb("w_raw", [P, 4, P])
        w_attn = sb("w_attn", [P, 4, P])
        b_qkv = sb("b_qkv", [1, QD])
        b_out = sb("b_out", [1, P])

        x = sb("x", [P, NT, P])
        xn = sb("xn", [P, NT, P])
        xnT = sb("xnT", [P, NT * P])
        stats = sb("stats", [P, NT, 6])
        m_sum = sb("m_sum", [P, NT])
        m_dif = sb("m_dif", [P, NT])
        v_sum = sb("v_sum", [P, NT])
        v_dif = sb("v_dif", [P, NT])
        mean = sb("mean", [P, NT])
        var = sb("var", [P, NT])
        std = sb("std", [P, NT])
        rstd = sb("rstd", [P, NT])

        logit = sb("logit", [P, NT, E])
        beats = sb("beats", [P, NT, E, E])
        ties = sb("ties", [P, NT, E, E])
        rank = sb("rank", [P, NT, E])
        is_rank = sb("is_rank", [P, TOPK, NT, E])
        chosen = sb("chosen", [P, NT, E], BF16)
        more = sb("more", [P, E, NT])
        tiles_of = sb("tiles_of", [P, E])
        below = sb("below", [P, E, E])
        first_tile = sb("first_tile", [P, E])
        end_tile = sb("end_tile", [P, E])
        past = sb("past", [P, NS, E])
        expert_f = sb("expert_f", [P, NS])
        expert_w = sb("expert_w", [P, NS], I32)
        expert_b = sb("expert_b", [P, NS], I32)
        slot = sb("slot", [P, NT, E])
        picked = sb("picked", [P, TOPK, NT, E])
        pos_i = sb("pos_i", [P, TOPK * NT], I32)
        hi_i = sb("hi_i", [P, TOPK * NT], I32)
        lo_i = sb("lo_i", [P, TOPK * NT], I32)
        hi_f = sb("hi_f", [P, TOPK * NT])
        lo_f = sb("lo_f", [P, TOPK * NT])
        lo_hot = sb("lo_hot", [P, TOPK * NT, P], BF16)
        hi_hot = sb("hi_hot", [P, TOPK * NT, NS], BF16)
        hi_val = sb("hi_val", [P, TOPK * NT, 2, NS], BF16)
        back = sb("back", [P, 2 * NS])
        row_f = sb("row_f", [P, NS])
        empty = sb("empty", [P, NS])
        dst_row = sb("dst_row", [P, NS], I32)
        src_row = sb("src_row", [P, NS], I32)
        top = sb("top", [P, TOPK, NT])
        gap = sb("gap", [P, NT])
        gap_exp = sb("gap_exp", [P, NT])
        gap_den = sb("gap_den", [P, NT])
        half_w = sb("half_w", [P, TOPK, NT])

        xg = sb("xg", [P, RING, P])
        xgT = sb("xgT", [P, RING, P])
        h_pre = sb("h_pre", [P, RING, DF])
        h_act = sb("h_act", [P, RING, DF])
        hT = sb("hT", [P, RING, DF])
        y_tile = sb("y_tile", [P, RING, P])
        y_back = sb("y_back", [P, TOPK, NT, P])

        xa = sb("xa", [P, 2, P])
        xaT = sb("xaT", [P, 2, P])
        neg = sb("neg", [P, 2, 2 * P])
        expo = sb("expo", [P, 2, 2 * P])
        qk = sb("qk", [P, 2, 2 * P])
        vx = sb("vx", [P, 2, H, VE])
        qT = sb("qT", [P, 2, P])
        kv = sb("kv", [P, 2, H * DH * VE])
        state = sb("state", [P, H * VE])
        prod = sb("prod", [P, H * DH * VE])
        local = sb("local", [P, H, VE])
        nd = sb("nd", [P, H, VE])
        den = sb("den", [P, H])
        rden = sb("rden", [P, H])
        merged = sb("merged", [P, 2, P])
        mT = sb("mT", [P, 2, P])

        xn_rows = [nc.dram_tensor(f"xn_rows{f}", [T, D], F32).ap() for f in range(2)]
        y_rows = [nc.dram_tensor(f"y_rows{f}", [TOPK * T, D], F32).ap() for f in range(2)]

        x_in = [sem(f"x_in{c}") for c in range(NC)]
        wg_in, w1_in, w2_in, b1_in, b2_in, attn_in = map(sem, ("wg_in", "w1_in", "w2_in", "b1_in", "b2_in", "attn_in"))
        const_step, consts = sem("const_step"), sem("consts")
        attn_w_ps, attn_w_sb = sem("attn_w_ps"), sem("attn_w_sb")
        dve_step = sem("dve_step")
        var_ready, std_ready = sem("var_ready"), sem("std_ready")
        xn_ready, xn_stored = sem("xn_ready"), sem("xn_stored")
        xnT_ps, xnT_sb, logits_ps = sem("xnT_ps"), sem("xnT_sb"), sem("logits_ps")
        chosen_ready, counts_ps = sem("chosen_ready"), sem("counts_ps")
        hot_ready, back_ps, table_ready = sem("hot_ready"), sem("back_ps"), sem("table_ready")
        gap_ready, gap_exp_ready = sem("gap_ready"), sem("gap_exp_ready")
        gathered = [sem(f"gathered{r}") for r in range(RING)]
        scattered = [sem(f"scattered{r}") for r in range(RING)]
        xg_ps, xg_sb, h_ps, h_biased, h_gelu = map(sem, ("xg_ps", "xg_sb", "h_ps", "h_biased", "h_gelu"))
        hT_ps, hT_sb, y_ps, y_sb = map(sem, ("hT_ps", "hT_sb", "y_ps", "y_sb"))
        y_loaded = [sem(f"y_loaded{c}") for c in range(NC)]
        xa_sb, xa_ps, xaT_sb, qkv_ps = map(sem, ("xa_sb", "xa_ps", "xaT_sb", "qkv_ps"))
        neg_sb, exp_sb, v_sb, phi_sb = map(sem, ("neg_sb", "exp_sb", "v_sb", "phi_sb"))
        qT_ps, qT_sb, kv_sb, prefix_ps = map(sem, ("qT_ps", "qT_sb", "kv_sb", "prefix_ps"))
        state_ps, state_sb = map(sem, ("state_ps", "state_sb"))
        prod_sb, local_sb, nd_sb, den_sb, rden_sb = map(sem, ("prod_sb", "local_sb", "nd_sb", "den_sb", "rden_sb"))
        merged_sb, m_ps, mT_sb, proj_ps, x_attn = map(sem, ("merged_sb", "m_ps", "mT_sb", "proj_ps", "x_attn"))
        x_final, out_stored = sem("x_final"), sem("out_stored")

        xg_bank = banks[:, 0, 0:P]
        y_bank = banks[:, 1, 0:P]
        def h_bank(r): return banks[:, 2 + r, :]
        def hT_bank(r): return banks[:, 5 + r, :]
        def xnT_bank(c): return banks[:, 2 + c, :]
        logit_bank = banks[:, 6, 0:NT * E]
        before_bank = banks[:, 7, 0:NT * E]
        count_bank = banks[:, 1, 0:E]
        back_bank = banks[:, 0, 0:2 * NS]
        prefix_bank = banks[:, 0:4, 0:H // 4 * DH * VE]
        qkv_bank = banks[:, 4, 0:QD]
        xa_bank, qT_bank, m_bank = (banks[:, 5, k * P:(k + 1) * P] for k in range(3))
        inter_bank = banks[:, 3, H // 4 * DH * VE:H // 4 * DH * VE + H * VE]
        proj_bank = banks[:, 6, 0:P]
        state_bank = banks[:, 7, 0:H * VE]

        def slots(eng, body):
            for r in range(RING):
                body(r, r)
            with eng.Fori(1, NS // RING - 1) as j:
                for r in range(RING):
                    body(j * RING + r, r)
            for r in range(RING):
                body(NS - RING + r, r)

        def tokens(eng, body):
            for i in range(2):
                body(i, i)
            with eng.Fori(1, NT // 2 - 1) as j:
                for r in range(2):
                    body(j * 2 + r, r)
            for i in (NT - 2, NT - 1):
                body(i, i % 2)

        block = ctx.enter_context(nc.Block())

        @block.sync
        def _(sp):
            x_v = x_d[0].rearrange("(t p) d -> p t d", p=P)
            for c in range(NC):
                sp.dma_start(x[:, c * CH:(c + 1) * CH, :], x_v[:, c * CH:(c + 1) * CH, :]).then_inc(x_in[c], 16)
            sp.dma_start(wg[:, :], Wg).then_inc(wg_in, 16)
            sp.dma_start(w1[:, :].rearrange("p (e f) -> p e f", e=E), W1.rearrange("e d f -> d e f")).then_inc(w1_in, 16)
            sp.dma_start(b1_all[:, :].rearrange("p (e f) -> p e f", e=E), b1.partition_broadcast(P)).then_inc(b1_in, 16)
            sp.dma_start(w2[:, :].rearrange("p (e n) -> p e n", n=P),
                         W2.rearrange("e (c p) d -> p (e c) d", p=P)).then_inc(w2_in, 16)
            sp.dma_start(b2_all[:, :].rearrange("p (e f) -> p e f", e=E), b2.partition_broadcast(P)).then_inc(b2_in, 16)
            for k, w in enumerate((Wq, Wk, Wv, Wo)):
                sp.dma_start(w_raw[:, k, :], w).then_inc(attn_in, 16)
            for k, b in enumerate((bq, bk, bv)):
                sp.dma_start(b_qkv[0:1, k * P:(k + 1) * P], b.rearrange("(a d) -> a d", a=1)).then_inc(attn_in, 16)
            sp.dma_start(b_out[:, :], bo.rearrange("(a d) -> a d", a=1)).then_inc(attn_in, 16)
            for f in range(2):
                rows = xn_rows[f].rearrange("(t p) d -> p t d", p=P)
                for c in range(NC):
                    sp.wait_ge(xn_ready, NT * f + CH * (c + 1))
                    sp.dma_start(rows[:, c * CH:(c + 1) * CH, :], xn[:, c * CH:(c + 1) * CH, :]).then_inc(xn_stored, 16)
                for r in range(RING):
                    sp.wait_ge(scattered[r], 16 * (NS // RING) * (f + 1))
                back_rows = y_rows[f].rearrange("(k t p) d -> k p t d", k=TOPK, p=P)
                for c in range(NC):
                    for k in range(TOPK):
                        sp.dma_start(y_back[:, k, c * CH:(c + 1) * CH, :],
                                     back_rows[k, :, c * CH:(c + 1) * CH, :]).then_inc(y_loaded[c], 16)
            out_v = out_d[0].rearrange("(t p) d -> p t d", p=P)
            for c in range(NC):
                sp.wait_ge(x_final, CH * (c + 1))
                sp.dma_start(out_v[:, c * CH:(c + 1) * CH, :], x[:, c * CH:(c + 1) * CH, :]).then_inc(out_stored, 16)
            sp.wait_ge(out_stored, 16 * NC)

        @block.gpsimd
        def _(pool):
            g = nc.gpsimd
            g.memset(ident[:, :], 0.0).then_inc(const_step, 1)
            g.memset(tri[:, :], 1.0).then_inc(const_step, 1)
            g.memset(strict_bf[:, :], 1.0).then_inc(const_step, 1)
            g.memset(before[:, :, :], 1.0).then_inc(const_step, 1)
            g.memset(head_mask[:, :, :], 1.0).then_inc(const_step, 1)
            pool.wait_ge(const_step, 5)
            g.affine_select(out=ident[:, :], in_=ident[:, :], compare_op=ALU.not_equal, fill=1.0, base=0,
                            pattern=[[-1, P]], channel_multiplier=1).then_inc(consts, 1)
            g.memset(ones_bf[:, :], 1.0).then_inc(consts, 1)
            g.memset(ones_row[:, :], 1.0).then_inc(consts, 1)
            g.affine_select(out=before[:, :, :], in_=before[:, :, :], compare_op=ALU.is_ge, fill=0.0, base=-1,
                            pattern=[[1, E], [-1, E]], channel_multiplier=0).then_inc(consts, 1)
            g.affine_select(out=strict_bf[:, :], in_=strict_bf[:, :], compare_op=ALU.is_ge, fill=0.0, base=-1,
                            pattern=[[1, P]], channel_multiplier=-1).then_inc(consts, 1)
            flt = dict(allow_small_or_imprecise_dtypes=True)
            g.iota(slot_no[:, :], pattern=[[1, NS]], base=0, channel_multiplier=0, **flt).then_inc(consts, 1)
            g.iota(lane_no[:, :], pattern=[[1, P]], base=0, channel_multiplier=0, **flt).then_inc(consts, 1)
            g.iota(full_tiles[:, :], pattern=[[P, NT]], base=0, channel_multiplier=0, **flt).then_inc(consts, 1)
            g.iota(pair_no[:, :], pattern=[[1, TOPK * NT]], base=1, channel_multiplier=0, **flt).then_inc(consts, 1)
            g.iota(own_lane[:, :], pattern=[[0, 1]], base=0, channel_multiplier=1, **flt).then_inc(consts, 1)
            g.affine_select(out=tri[:, :], in_=tri[:, :], compare_op=ALU.is_ge, fill=0.0, base=0,
                            pattern=[[1, P]], channel_multiplier=-1).then_inc(consts, 1)
            g.affine_select(out=head_mask[:, :, :], in_=head_mask[:, :, :], compare_op=ALU.is_ge, fill=0.0, base=0,
                            pattern=[[-DH, H], [0, VE]], channel_multiplier=1).then_inc(const_step, 1)
            pool.wait_ge(const_step, 6)
            g.affine_select(out=head_mask[:, :, :], in_=head_mask[:, :, :], compare_op=ALU.is_ge, fill=0.0,
                            base=DH - 1, pattern=[[DH, H], [0, VE]], channel_multiplier=-1).then_inc(consts, 1)
            g.memset(vx[:, :, :, :], 1.0).then_inc(consts, 1)
            g.memset(state[:, :], 0.0).then_inc(consts, 1)

            def ffn_moves(f):
                pool.wait_ge(xn_stored, 16 * NC * (f + 1))
                pool.wait_ge(table_ready, f + 1)
                lag = 5
                for n in range(NS + lag):
                    if n < NS:
                        at_least(pool, xg_ps, NS * f + n - RING + 1)
                        g.indirect_dma_start(
                            out=xg[:, n % RING, :], out_offset=None, in_=xn_rows[f][:, :],
                            in_offset=bass.IndirectOffsetOnAxis(ap=src_row[:, n:n + 1], axis=0),
                        ).then_inc(gathered[n % RING], 16)
                    i = n - lag
                    if i >= 0:
                        pool.wait_ge(y_sb, NS * f + i + 1)
                        g.indirect_dma_start(
                            out=y_rows[f][:, :],
                            out_offset=bass.IndirectOffsetOnAxis(ap=dst_row[:, i:i + 1], axis=0),
                            in_=y_tile[:, i % RING, :], in_offset=None,
                            bounds_check=TOPK * T - 1, oob_is_err=False,
                        ).then_inc(scattered[i % RING], 16)

            ffn_moves(0)

            def outer(i, r):
                pool.wait_ge(phi_sb, i + 1)
                pool.wait_ge(v_sb, i + 1)
                at_least(pool, prefix_ps, i - 1)
                k4 = qk[:, r, P:2 * P].rearrange("p (h d) -> p h d", h=H).unsqueeze(3).to_broadcast([P, H, DH, VE])
                v4 = vx[:, r, :, :].unsqueeze(2).to_broadcast([P, H, DH, VE])
                o4 = kv[:, r, :].rearrange("p (h d e) -> p h d e", h=H, d=DH)
                g.tensor_tensor(o4, k4, v4, ALU.mult).then_inc(kv_sb, 1)

            tokens(pool, outer)
            ffn_moves(1)

        @block.scalar
        def _(act):
            s = nc.scalar

            def ln_std(k):
                act.wait_ge(var_ready, k + 1)
                s.activation(std[:, :], var[:, :], ACT.Sqrt).then_inc(std_ready, 1)

            def ffn(f):
                ln_std(2 * f)
                for c in range(NC):
                    act.wait_ge(xnT_ps, NC * f + c + 1)
                    s.copy(xnT[:, c * CH * P:(c + 1) * CH * P], xnT_bank(c)).then_inc(xnT_sb, 1)
                act.wait_ge(gap_ready, f + 1)
                s.activation(gap_exp[:, :], gap[:, :], ACT.Exp).then_inc(gap_exp_ready, 1)
                base = NS * f

                def skewed(i, r):
                    act.wait_ge(xg_ps, base + i + 1)
                    at_least(act, h_ps, base + i - RING + 1)
                    s.copy(xgT[:, r, :], xg_bank).then_inc(xg_sb, 1)
                    if not (isinstance(i, int) and i == 0):
                        q = (r - 1) % RING
                        act.wait_ge(hT_ps, base + i)
                        at_least(act, y_ps, base + i - RING)
                        s.copy(hT[:, q, :], hT_bank(q)).then_inc(hT_sb, 1)
                    act.wait_ge(h_biased, base + i + 1)
                    at_least(act, hT_ps, base + i - RING + 1)
                    s.activation(h_act[:, r, :], h_pre[:, r, :], ACT.Gelu_apprx_tanh).then_inc(h_gelu, 1)

                slots(act, skewed)
                q = (NS - 1) % RING
                act.wait_ge(hT_ps, base + NS)
                act.wait_ge(y_ps, base + NS - RING)
                s.copy(hT[:, q, :], hT_bank(q)).then_inc(hT_sb, 1)

            act.wait_ge(attn_w_ps, 1)
            s.copy(w_attn[:, :, :].rearrange("p k n -> p (k n)"), banks[:, 5, :]).then_inc(attn_w_sb, 1)
            ffn(0)
            ln_std(1)

            def pre(i, r):
                act.wait_ge(xa_ps, i + 1)
                at_least(act, qkv_ps, i - 1)
                s.copy(xaT[:, r, :], xa_bank).then_inc(xaT_sb, 1)
                act.wait_ge(qkv_ps, i + 1)
                at_least(act, exp_sb, i - 1)
                s.activation(neg[:, r, :], qkv_bank[:, 0:2 * P], ACT.Relu, scale=-1.0).then_inc(neg_sb, 1)
                at_least(act, kv_sb, i - 1)
                at_least(act, state_ps, i - 1)
                s.copy(vx[:, r, :, 0:DH], qkv_bank[:, 2 * P:QD].rearrange("p (h d) -> p h d", h=H)).then_inc(v_sb, 1)
                act.wait_ge(neg_sb, i + 1)
                at_least(act, phi_sb, i - 1)
                s.activation(expo[:, r, :], neg[:, r, :], ACT.Exp, scale=-1.0).then_inc(exp_sb, 1)

            def post(i, r):
                act.wait_ge(m_ps, i + 1)
                at_least(act, proj_ps, i - 1)
                s.copy(mT[:, r, :], m_bank).then_inc(mT_sb, 1)

            act.wait_ge(consts, 14)
            pre(0, 0)
            pre(1, 1)

            def attn(i, r, lead=True):
                act.wait_ge(qT_ps, i + 1)
                at_least(act, prefix_ps, i - 1)
                s.copy(qT[:, r, :], qT_bank).then_inc(qT_sb, 1)
                if lead:
                    pre(i + 2, r)
                if not (isinstance(i, int) and i == 0):
                    post(i - 1, 1 - r)

            for i in range(2):
                attn(i, i)
            with act.Fori(1, NT // 2 - 1) as j:
                for r in range(2):
                    attn(2 * j + r, r)
            for i in (NT - 2, NT - 1):
                attn(i, i % 2, lead=False)
            post(NT - 1, (NT - 1) % 2)
            ffn(1)

        @block.vector
        def _(dve):
            v = nc.vector
            steps = [0]

            def link(ins):
                steps[0] += 1
                ins.then_inc(dve_step, 1)
                dve.wait_ge(dve_step, steps[0])

            def ln_moments(k):
                me, mo = stats[:, :, 1], stats[:, :, 4]
                v.tensor_tensor(m_sum[:, :], me, mo, ALU.add).then_inc(dve_step, 1)
                v.tensor_tensor(v_sum[:, :], stats[:, :, 2], stats[:, :, 5], ALU.add).then_inc(dve_step, 1)
                steps[0] += 2
                link(v.tensor_tensor(m_dif[:, :], me, mo, ALU.subtract))
                v.tensor_scalar(mean[:, :], m_sum[:, :], 0.5, None, ALU.mult).then_inc(dve_step, 1)
                steps[0] += 1
                link(v.scalar_tensor_tensor(out=v_dif[:, :], in0=m_dif[:, :], scalar=0.25, in1=m_dif[:, :],
                                            op0=ALU.mult, op1=ALU.mult))
                link(v.scalar_tensor_tensor(out=v_dif[:, :], in0=v_sum[:, :], scalar=1.0 / D, in1=v_dif[:, :],
                                            op0=ALU.mult, op1=ALU.add))
                v.tensor_scalar(var[:, :], v_dif[:, :], LN_EPS, None, ALU.add).then_inc(var_ready, 1)
                dve.wait_ge(std_ready, k + 1)
                link(v.reciprocal(rstd[:, :], std[:, :]))

            def gate_and_route(f):
                for t in range(NT):
                    v.tensor_scalar(xn[:, t, :], x[:, t, :], mean[:, t:t + 1], rstd[:, t:t + 1],
                                    ALU.subtract, ALU.mult).then_inc(xn_ready, 1)
                dve.wait_ge(logits_ps, f + 1)
                link(v.tensor_copy(logit[:, :, :].rearrange("p t e -> p (t e)"), logit_bank))
                if f == 0:
                    dve.wait_ge(consts, 14)
                mine = logit[:, :, :].unsqueeze(3).to_broadcast([P, NT, E, E])
                other = logit[:, :, :].unsqueeze(2).to_broadcast([P, NT, E, E])
                v.tensor_tensor(beats[:, :, :, :], other, mine, ALU.is_gt).then_inc(dve_step, 1)
                steps[0] += 1
                link(v.tensor_tensor(ties[:, :, :, :], other, mine, ALU.is_equal))
                link(v.tensor_tensor(ties[:, :, :, :], ties[:, :, :, :],
                                     before[:, :, :].unsqueeze(1).to_broadcast([P, NT, E, E]), ALU.mult))
                link(v.tensor_tensor(beats[:, :, :, :], beats[:, :, :, :], ties[:, :, :, :], ALU.add))
                link(v.tensor_reduce(rank[:, :, :], beats[:, :, :, :], AX.X, ALU.add))
                v.tensor_scalar(chosen[:, :, :], rank[:, :, :], float(TOPK), None, ALU.is_lt).then_inc(chosen_ready, 1)
                v.tensor_scalar(is_rank[:, 0, :, :], rank[:, :, :], 0.0, None, ALU.is_equal).then_inc(dve_step, 1)
                steps[0] += 1
                link(v.tensor_scalar(is_rank[:, 1, :, :], rank[:, :, :], 1.0, None, ALU.is_equal))
                both = logit[:, :, :].unsqueeze(1).to_broadcast([P, TOPK, NT, E])
                link(v.tensor_tensor(picked[:, :, :, :], is_rank[:, :, :, :], both, ALU.mult))
                link(v.tensor_reduce(top[:, :, :], picked[:, :, :, :], AX.X, ALU.add))
                v.tensor_tensor(gap[:, :], top[:, 1, :], top[:, 0, :], ALU.subtract).then_inc(gap_ready, 1)
                dve.wait_ge(counts_ps, f + 1)
                link(v.tensor_copy(tiles_of[:, :], count_bank))
                link(v.tensor_tensor(more[:, :, :], tiles_of[:, :].unsqueeze(2).to_broadcast([P, E, NT]),
                                     full_tiles[:, :].unsqueeze(1).to_broadcast([P, E, NT]), ALU.is_gt))
                link(v.tensor_reduce(tiles_of[:, :], more[:, :, :], AX.X, ALU.add))
                link(v.tensor_tensor(below[:, :, :], before[:, :, :],
                                     tiles_of[:, :].unsqueeze(1).to_broadcast([P, E, E]), ALU.mult))
                link(v.tensor_reduce(first_tile[:, :], below[:, :, :], AX.X, ALU.add))
                v.tensor_tensor(end_tile[:, :], first_tile[:, :], tiles_of[:, :], ALU.add).then_inc(dve_step, 1)
                steps[0] += 1
                link(v.tensor_scalar(first_tile[:, :], first_tile[:, :], float(P), None, ALU.mult))
                link(v.tensor_tensor(slot[:, :, :], before_bank.rearrange("p (t e) -> p t e", e=E),
                                     first_tile[:, :].unsqueeze(1).to_broadcast([P, NT, E]), ALU.add))
                link(v.tensor_tensor(picked[:, :, :, :], is_rank[:, :, :, :],
                                     slot[:, :, :].unsqueeze(1).to_broadcast([P, TOPK, NT, E]), ALU.mult))
                with nc.allow_low_precision(reason="whole numbers below 2 ** 24, summed in float32"):
                    link(v.tensor_reduce(pos_i[:, :], picked[:, :, :, :].rearrange("p k t e -> p (k t) e"),
                                         AX.X, ALU.add))
                v.tensor_scalar(hi_i[:, :], pos_i[:, :], 7, None, ALU.logical_shift_right).then_inc(dve_step, 1)
                steps[0] += 1
                link(v.tensor_scalar(lo_i[:, :], pos_i[:, :], P - 1, None, ALU.bitwise_and))
                v.tensor_copy(hi_f[:, :], hi_i[:, :]).then_inc(dve_step, 1)
                steps[0] += 1
                link(v.tensor_copy(lo_f[:, :], lo_i[:, :]))
                KT = TOPK * NT
                link(v.tensor_tensor(hi_hot[:, :, :], slot_no[:, :].unsqueeze(1).to_broadcast([P, KT, NS]),
                                     hi_f[:, :].unsqueeze(2).to_broadcast([P, KT, NS]), ALU.is_equal))
                v.tensor_scalar(hi_val[:, :, 0, :], hi_hot[:, :, :], own_lane[:, 0:1], None,
                                ALU.mult).then_inc(hot_ready, 1)
                v.tensor_tensor(hi_val[:, :, 1, :], hi_hot[:, :, :],
                                pair_no[:, :].unsqueeze(2).to_broadcast([P, KT, NS]), ALU.mult).then_inc(hot_ready, 1)
                for q in range(KT):
                    v.tensor_scalar(lo_hot[:, q, :], lane_no[:, :], lo_f[:, q:q + 1], None,
                                    ALU.is_equal).then_inc(hot_ready, 1)
                link(v.tensor_tensor(past[:, :, :], slot_no[:, :].unsqueeze(2).to_broadcast([P, NS, E]),
                                     end_tile[:, :].unsqueeze(1).to_broadcast([P, NS, E]), ALU.is_ge))
                link(v.tensor_reduce(expert_f[:, :], past[:, :, :], AX.X, ALU.add))
                v.tensor_scalar(expert_w[:, :], expert_f[:, :], float(E - 1), float(DF), ALU.min, ALU.mult).then_inc(dve_step, 1)
                steps[0] += 1
                link(v.tensor_scalar(expert_b[:, :], expert_f[:, :], float(E - 1), float(D), ALU.min, ALU.mult))
                dve.wait_ge(back_ps, f + 1)
                link(v.tensor_copy(back[:, :], back_bank))
                v.tensor_scalar(empty[:, :], back[:, NS:2 * NS], 0.0, float(PAD), ALU.is_equal, ALU.mult).then_inc(dve_step, 1)
                steps[0] += 1
                link(v.scalar_tensor_tensor(out=row_f[:, :], in0=back[:, NS:2 * NS], scalar=float(P), in1=back[:, 0:NS],
                                            op0=ALU.mult, op1=ALU.add))
                link(v.scalar_tensor_tensor(out=dst_row[:, :], in0=row_f[:, :], scalar=-float(P), in1=empty[:, :],
                                            op0=ALU.add, op1=ALU.add))
                v.tensor_scalar(src_row[:, :], dst_row[:, :], T - 1, None, ALU.bitwise_and).then_inc(table_ready, 1)
                dve.wait_ge(gap_exp_ready, f + 1)
                link(v.tensor_scalar(gap_den[:, :], gap_exp[:, :], 1.0, 2.0, ALU.add, ALU.mult))
                link(v.reciprocal(half_w[:, 0, :], gap_den[:, :]))
                link(v.tensor_tensor(half_w[:, 1, :], half_w[:, 0, :], gap_exp[:, :], ALU.mult))

            def experts(f):
                base = NS * f
                if f == 0:
                    dve.wait_ge(b1_in, 16)
                    dve.wait_ge(b2_in, 16)

                def hidden(i, r):
                    col = dve.value_load(expert_w[0:1, bass.ds(i, 1)], min_val=0, max_val=(E - 1) * DF)
                    dve.wait_ge(h_ps, base + i + 1)
                    at_least(dve, h_gelu, base + i - RING + 1)
                    v.tensor_tensor(h_pre[:, r, :], h_bank(r), b1_all[:, bass.ds(col, DF)], ALU.add).then_inc(h_biased, 1)

                def output(i, r):
                    col = dve.value_load(expert_b[0:1, bass.ds(i, 1)], min_val=0, max_val=(E - 1) * D)
                    dve.wait_ge(y_ps, base + i + 1)
                    if isinstance(i, int):
                        at_least(dve, scattered[r], 16 * ((base + i) // RING))
                    else:
                        dve.wait_ge(scattered[r], (base + i - r) // RING * 16)
                    v.tensor_tensor(y_tile[:, r, :], y_bank, b2_all[:, bass.ds(col, D)], ALU.add).then_inc(y_sb, 1)

                LAG = 2
                for i in range(RING):
                    hidden(i, i)
                    if i >= LAG:
                        output(i - LAG, i - LAG)
                with dve.Fori(1, NS // RING) as j:
                    for r in range(RING):
                        hidden(j * RING + r, r)
                        q = (r - LAG) % RING
                        i = j * RING + r - LAG
                        col = dve.value_load(expert_b[0:1, bass.ds(i, 1)], min_val=0, max_val=(E - 1) * D)
                        dve.wait_ge(y_ps, base + i + 1)
                        done = j if r >= LAG else j - 1
                        dve.wait_ge(scattered[q], done * 16 + 16 * (NS // RING) * f)
                        v.tensor_tensor(y_tile[:, q, :], y_bank, b2_all[:, bass.ds(col, D)], ALU.add).then_inc(y_sb, 1)
                for i in range(NS - LAG, NS):
                    output(i, i % RING)

            def combine(f):
                for t in range(NT):
                    if t % CH == 0:
                        dve.wait_ge(y_loaded[t // CH], 16 * TOPK * (f + 1))
                    v.scalar_tensor_tensor(out=y_back[:, 0, t, :], in0=y_back[:, 0, t, :],
                                           scalar=half_w[:, 0, t:t + 1], in1=x[:, t, :],
                                           op0=ALU.mult, op1=ALU.add).then_inc(dve_step, 1)
                first = steps[0]
                steps[0] += NT
                for t in range(NT):
                    dve.wait_ge(dve_step, first + t + 1)
                    v.scalar_tensor_tensor(out=x[:, t, :], in0=y_back[:, 1, t, :],
                                           scalar=half_w[:, 1, t:t + 1], in1=y_back[:, 0, t, :],
                                           op0=ALU.mult, op1=ALU.add).then_inc(x_final if f else dve_step, 1)
                if f == 0:
                    second = steps[0]
                    steps[0] += NT
                    for t in range(NT):
                        dve.wait_ge(dve_step, second + t + 1)
                        v.bn_stats(stats[:, t, :], x[:, t, :]).then_inc(dve_step, 1)
                    steps[0] += NT
                    dve.wait_ge(dve_step, steps[0])

            for t in range(NT):
                if t % CH == 0:
                    dve.wait_ge(x_in[t // CH], 16)
                v.bn_stats(stats[:, t, :], x[:, t, :]).then_inc(dve_step, 1)
            steps[0] += NT
            dve.wait_ge(dve_step, steps[0])
            ln_moments(0)
            gate_and_route(0)
            experts(0)
            combine(0)
            ln_moments(1)

            def norm(i, r):
                at_least(dve, xa_ps, i - 1)
                v.tensor_scalar(xa[:, r, :], x[:, bass.ds(i, 1), :].rearrange("p a d -> p (a d)"),
                                mean[:, bass.ds(i, 1)], rstd[:, bass.ds(i, 1)],
                                ALU.subtract, ALU.mult).then_inc(xa_sb, 1)

            def phi(i, r):
                dve.wait_ge(exp_sb, i + 1)
                at_least(dve, local_sb, i - 1)
                at_least(dve, kv_sb, i - 1)
                at_least(dve, state_ps, i - 1)
                v.scalar_tensor_tensor(out=qk[:, r, :], in0=qkv_bank[:, 0:2 * P], scalar=0.0, in1=expo[:, r, :],
                                       op0=ALU.max, op1=ALU.add).then_inc(phi_sb, 1)

            def attend(i, r):
                dve.wait_ge(prefix_ps, i + 1)
                at_least(dve, local_sb, i)
                q4 = qk[:, r, 0:P].rearrange("p (b n) -> p b n", b=4).unsqueeze(3).to_broadcast([P, 4, P // 4, VE])
                v.tensor_tensor(prod[:, :].rearrange("p (b n e) -> p b n e", b=4, e=VE),
                                prefix_bank.rearrange("p b (n e) -> p b n e", e=VE), q4, ALU.mult).then_inc(prod_sb, 1)
                dve.wait_ge(prod_sb, i + 1)
                at_least(dve, nd_sb, i)
                v.tensor_reduce(local[:, :, :], prod[:, :].rearrange("p (h d e) -> p h e d", h=H, d=DH),
                                AX.X, ALU.add).then_inc(local_sb, 1)
                dve.wait_ge(local_sb, i + 1)
                v.tensor_tensor(nd[:, :, :], inter_bank.rearrange("p (h e) -> p h e", h=H), local[:, :, :],
                                ALU.add).then_inc(nd_sb, 1)
                dve.wait_ge(state_ps, i + 1)
                v.tensor_tensor(state[:, :], state_bank, head_mask[:, :, :].rearrange("p h e -> p (h e)"),
                                ALU.mult).then_inc(state_sb, 1)
                dve.wait_ge(nd_sb, i + 1)
                v.tensor_scalar(den[:, :], nd[:, :, DH], ATT_EPS, None, ALU.add).then_inc(den_sb, 1)
                dve.wait_ge(den_sb, i + 1)
                v.reciprocal(rden[:, :], den[:, :]).then_inc(rden_sb, 1)
                dve.wait_ge(rden_sb, i + 1)
                at_least(dve, m_ps, i - 1)
                v.tensor_tensor(merged[:, r, :].rearrange("p (h d) -> p h d", h=H), nd[:, :, 0:DH],
                                rden[:, :].unsqueeze(2).to_broadcast([P, H, DH]), ALU.mult).then_inc(merged_sb, 1)

            def residual(i):
                dve.wait_ge(proj_ps, i + 1)
                xt = x[:, bass.ds(i, 1), :].rearrange("p a d -> p (a d)")
                v.tensor_tensor(xt, proj_bank, xt, ALU.add).then_inc(x_attn, 1)

            norm(0, 0)
            norm(1, 1)
            phi(0, 0)

            def attn(i, r, norms=True, phis=True):
                if norms:
                    norm(i + 2, r)
                if phis:
                    phi(i + 1, 1 - r)
                attend(i, r)
                if not (isinstance(i, int) and i == 0):
                    residual(i - 1)

            for i in range(2):
                attn(i, i)
            with dve.Fori(1, NT // 2 - 1) as j:
                for r in range(2):
                    attn(2 * j + r, r)
            attn(NT - 2, 0, norms=False)
            attn(NT - 1, 1, norms=False, phis=False)
            residual(NT - 1)

            dve.wait_ge(x_attn, NT)
            for t in range(NT):
                v.bn_stats(stats[:, t, :], x[:, t, :]).then_inc(dve_step, 1)
            steps[0] += NT
            dve.wait_ge(dve_step, steps[0])
            ln_moments(2)
            gate_and_route(1)
            experts(1)
            combine(1)

        @block.tensor
        def _(pe):
            mm = nc.tensor.matmul
            pe.wait_ge(consts, 14)

            def gate(f):
                for c in range(NC):
                    for t in range(c * CH, (c + 1) * CH):
                        pe.wait_ge(xn_ready, NT * f + t + 1)
                        last = pe.transpose(xnT_bank(c)[:, (t % CH) * P:(t % CH + 1) * P], xn[:, t, :], ident[:, :])
                    last.then_inc(xnT_ps, 1)
                if f == 0:
                    pe.wait_ge(wg_in, 16)
                for t in range(NT):
                    pe.wait_ge(xnT_sb, NC * f + t // CH + 1)
                    last = mm(logit_bank[:, t * E:(t + 1) * E], xnT[:, t * P:(t + 1) * P], wg[:, :],
                              start=True, stop=True)
                last.then_inc(logits_ps, 1)

            def route(f):
                pe.wait_ge(chosen_ready, f + 1)
                for t in range(NT):
                    mm(count_bank, ones_bf[:, :], chosen[:, t, :], start=(t == 0), stop=(t == NT - 1))
                for t in range(NT - 1):
                    left = NT - 1 - t
                    mm(before_bank[:, (t + 1) * E:], ones_bf[:, :],
                       chosen[:, t, :].unsqueeze(1).to_broadcast([P, left, E]), start=(t == 0),
                       stop=False, skip_group_check=True)
                last = mm(before_bank, strict_bf[:, :], chosen[:, :, :].rearrange("p t e -> p (t e)"),
                          start=False, stop=True, skip_group_check=True)
                last.then_inc(counts_ps, 1)
                KT = TOPK * NT
                for q in range(KT):
                    pe.wait_ge(hot_ready, (KT + 2) * f + 2 + q + 1)
                    last = mm(back_bank, lo_hot[:, q, :], hi_val[:, q, :, :].rearrange("p a s -> p (a s)"),
                              start=(q == 0), stop=(q == KT - 1))
                last.then_inc(back_ps, 1)

            def experts(f):
                base = NS * f
                pe.wait_ge(table_ready, f + 1)
                if f == 0:
                    pe.wait_ge(w1_in, 16)
                    pe.wait_ge(w2_in, 16)

                def hidden(i, r):
                    col = pe.value_load(expert_w[0:1, bass.ds(i, 1)], min_val=0, max_val=(E - 1) * DF)
                    pe.wait_ge(xg_sb, base + i + 1)
                    at_least(pe, h_biased, base + i - RING + 1)
                    mm(h_bank(r), xgT[:, r, :], w1[:, bass.ds(col, DF)], start=True, stop=True).then_inc(h_ps, 1)

                def turn(i, r):
                    pe.wait_ge(h_gelu, base + i + 1)
                    at_least(pe, hT_sb, base + i - RING + 1)
                    for c in range(FC):
                        last = pe.transpose(hT_bank(r)[:, c * P:(c + 1) * P], h_act[:, r, c * P:(c + 1) * P], ident[:, :])
                    last.then_inc(hT_ps, 1)

                def output(i, r):
                    col = pe.value_load(expert_w[0:1, bass.ds(i, 1)], min_val=0, max_val=(E - 1) * DF)
                    pe.wait_ge(hT_sb, base + i + 1)
                    at_least(pe, y_sb, base + i)
                    for c in range(FC):
                        last = mm(y_bank, hT[:, r, c * P:(c + 1) * P], w2[:, bass.ds(col + c * P, P)],
                                  start=(c == 0), stop=(c == FC - 1))
                    last.then_inc(y_ps, 1)

                def transposed_rows(j, r, ahead):
                    slot_r = (r + ahead) % RING
                    fills = j + (r + ahead) // RING + 1
                    pe.wait_ge(gathered[slot_r], fills * 16 + 16 * (NS // RING) * f)
                    at_least(pe, xg_sb, base + j * RING + r + ahead)
                    pe.transpose(xg_bank, xg[:, slot_r, :], ident[:, :]).then_inc(xg_ps, 1)

                def step(j, r, last=False):
                    i = j * RING + r
                    if not (last and r + 2 >= RING):
                        transposed_rows(j, r, 2)
                    if not (last and r + 1 >= RING):
                        hidden(i + 1, (r + 1) % RING)
                    if not (isinstance(i, int) and i == 0):
                        output(i - 1, (r - 1) % RING)
                    turn(i, r)

                transposed_rows(0, 0, 0)
                transposed_rows(0, 1, 0)
                hidden(0, 0)
                for r in range(RING):
                    step(0, r)
                with pe.Fori(1, NS // RING - 1) as j:
                    for r in range(RING):
                        step(j, r)
                for r in range(RING):
                    step(NS // RING - 1, r, last=True)
                output(NS - 1, (NS - 1) % RING)

            pe.wait_ge(attn_in, 16 * 8)
            for k in range(4):
                last = pe.transpose(banks[:, 5, k * P:(k + 1) * P], w_raw[:, k, :], ident[:, :])
            last.then_inc(attn_w_ps, 1)
            pe.wait_ge(attn_w_sb, 1)
            gate(0)
            route(0)
            experts(0)

            wqkv = w_attn[:, 0:3, :].rearrange("p k n -> p (k n)")

            def project(i, r):
                pe.wait_ge(xa_sb, i + 1)
                at_least(pe, xaT_sb, i)
                at_least(pe, qT_sb, i - 1)
                at_least(pe, mT_sb, i - 3)
                pe.transpose(xa_bank, xa[:, r, :], ident[:, :]).then_inc(xa_ps, 1)
                at_least(pe, phi_sb, i)
                at_least(pe, exp_sb, i)
                mm(qkv_bank, ones_row[:, :], b_qkv[:, :], start=True, stop=False)
                pe.wait_ge(xaT_sb, i + 1)
                mm(qkv_bank, xaT[:, r, :], wqkv, start=False, stop=True).then_inc(qkv_ps, 1)

            def out_proj(i, r, lead=True, last=False):
                pe.wait_ge(merged_sb, i + 1)
                at_least(pe, mT_sb, i)
                pe.wait_ge(qT_sb, i + 2 if not last else NT)
                pe.wait_ge(xaT_sb, i + 4 if lead else NT)
                pe.transpose(m_bank, merged[:, r, :], ident[:, :]).then_inc(m_ps, 1)
                at_least(pe, x_attn, i)
                mm(proj_bank, ones_row[:, :], b_out[:, :], start=True, stop=False)
                pe.wait_ge(mT_sb, i + 1)
                mm(proj_bank, mT[:, r, :], w_attn[:, 3, :], start=False, stop=True).then_inc(proj_ps, 1)

            def attn(i, r, lead=True):
                pe.wait_ge(phi_sb, i + 1)
                pe.wait_ge(xaT_sb, i + 2 if lead else NT)
                at_least(pe, mT_sb, i - 1)
                pe.transpose(qT_bank, qk[:, r, 0:P], ident[:, :]).then_inc(qT_ps, 1)
                pe.wait_ge(kv_sb, i + 1)
                at_least(pe, nd_sb, i)
                n = H // 4 * DH * VE
                for b in range(4):
                    mm(prefix_bank[:, b, :], tri[:, :], kv[:, r, b * n:(b + 1) * n], start=True, stop=True)
                pe.wait_ge(qT_sb, i + 1)
                if not (isinstance(i, int) and i == 0):
                    pe.wait_ge(state_sb, i)
                mm(inter_bank, qT[:, r, :], state[:, :], start=True, stop=True).then_inc(prefix_ps, 1)
                mm(state_bank, qk[:, r, P:2 * P], vx[:, r, :, :].rearrange("p h e -> p (h e)"),
                   start=(isinstance(i, int) and i == 0), stop=True, skip_group_check=True).then_inc(state_ps, 1)
                if lead:
                    project(i + 2, r)
                if not (isinstance(i, int) and i == 0):
                    out_proj(i - 1, 1 - r, lead)

            project(0, 0)
            project(1, 1)
            for i in range(2):
                attn(i, i)
            with pe.Fori(1, NT // 2 - 1) as j:
                for r in range(2):
                    attn(2 * j + r, r)
            for i in (NT - 2, NT - 1):
                attn(i, i % 2, lead=False)
            out_proj(NT - 1, (NT - 1) % 2, lead=False, last=True)
            gate(1)
            route(1)
            experts(1)


_INS = ['L0_attn_x', 'L0_attn_Wq', 'L0_attn_bq', 'L0_attn_Wk', 'L0_attn_bk', 'L0_attn_Wv', 'L0_attn_bv',
        'L0_attn_Wo', 'L0_attn_bo', 'L0_ffn_Wg', 'L0_ffn_W1', 'L0_ffn_b1', 'L0_ffn_W2', 'L0_ffn_b2']


def kernel(**inputs):
    import numpy as _np
    import concourse.bacc as _bacc
    from concourse import mybir as _mybir
    from concourse.bass_utils import run_bass_kernel_spmd as _run

    nc = _bacc.Bacc("TRN2", target_bir_lowering=False, num_devices=1)
    arrays, args = {}, []
    for name in _INS:
        a = _np.ascontiguousarray(inputs[name])
        arrays[f"in_{name}"] = a
        args.append(nc.dram_tensor(f"in_{name}", a.shape, _mybir.dt.from_np(a.dtype), kind="ExternalInput").ap())
    shape = inputs['L0_attn_x'].shape
    out = nc.dram_tensor("out_0", shape, _mybir.dt.float32, kind="ExternalOutput").ap()
    macaron_kernel(nc, *args, out)
    r = _run(nc, [arrays], core_ids=[0])
    return r.results[0]["out_0"]
```

```python
from contextlib import ExitStack

import concourse.bass as bass
from concourse import mybir

F32 = mybir.dt.float32
BF16 = mybir.dt.bfloat16
I32 = mybir.dt.int32
U32 = mybir.dt.uint32
ALU = mybir.AluOpType
ACT = mybir.ActivationFunctionType
AX = mybir.AxisListType

P = 128
RING = 3


def at_least(eng, sem, value):
    if isinstance(value, int) and value <= 0:
        return
    eng.wait_ge(sem, value)


def macaron_kernel(nc, x_d, Wq, bq, Wk, bk, Wv, bv, Wo, bo, Wg, W1b, W2, b2, out_d):
    T, D = x_d.shape[1], x_d.shape[2]
    E, DF = W2.shape[0], W2.shape[1]
    H, DH = 16, D // 16
    NT = T // P
    FC = DF // P
    TOPK = 2
    NS = (TOPK * T + E * (P - 1)) // P
    QD = 3 * D
    VE = DH + 1
    PAD = 2 * TOPK * T
    LN_EPS, ATT_EPS = 1e-5, 1e-6
    CH = 4
    NC = NT // CH
    assert D == P and NS % RING == 0 and T & (T - 1) == 0

    with ExitStack() as ctx:
        def sb(name, shape, dt=F32):
            return ctx.enter_context(nc.sbuf_tensor(name, shape, dt))

        def sem(name):
            return ctx.enter_context(nc.semaphore(name))

        banks = ctx.enter_context(nc.psum_tensor("banks", [P, 8, 512], F32))

        ident = sb("ident", [P, P])
        tri = sb("tri", [P, P])
        strict_bf = sb("strict_bf", [P, P], BF16)
        ones_bf = sb("ones_bf", [P, P], BF16)
        ones_row = sb("ones_row", [1, P])
        before = sb("before", [P, E, E])
        head_mask = sb("head_mask", [P, H, VE])
        slot_no = sb("slot_no", [P, NS])
        lane_no = sb("lane_no", [P, P])
        full_tiles = sb("full_tiles", [P, NT])
        pair_no = sb("pair_no", [P, TOPK * NT])
        own_lane = sb("own_lane", [P, 1])

        w2 = sb("w2", [P, E * DF])
        w1b = sb("w1b", [P, RING, DF + FC])
        b2_rep = sb("b2_rep", [P, P])
        b2_blk = sb("b2_blk", [P, NT, P])
        tile_mask = sb("tile_mask", [P, NT])
        wg = sb("wg", [P, E])
        w_raw = sb("w_raw", [P, 4, P])
        w_attn = sb("w_attn", [P, 4, P])
        b_qkv = sb("b_qkv", [1, QD])
        b_out = sb("b_out", [1, P])

        x = sb("x", [P, NT, P])
        xn = sb("xn", [P, NT, P])
        xnT = sb("xnT", [P, NT * P])
        stats = sb("stats", [P, NT, 6])
        m_sum = sb("m_sum", [P, NT])
        m_dif = sb("m_dif", [P, NT])
        v_sum = sb("v_sum", [P, NT])
        v_dif = sb("v_dif", [P, NT])
        mean = sb("mean", [P, NT])
        var = sb("var", [P, NT])
        std = sb("std", [P, NT])
        rstd = sb("rstd", [P, NT])

        logit = sb("logit", [P, NT, E])
        beats = sb("beats", [P, NT, E, E])
        ties = sb("ties", [P, NT, E, E])
        rank = sb("rank", [P, NT, E])
        is_rank = sb("is_rank", [P, TOPK, NT, E])
        chosen = sb("chosen", [P, NT, E], BF16)
        more = sb("more", [P, E, NT])
        tiles_of = sb("tiles_of", [P, E])
        below = sb("below", [P, E, E])
        first_tile = sb("first_tile", [P, E])
        end_tile = sb("end_tile", [P, E])
        past = sb("past", [P, NS, E])
        expert_f = sb("expert_f", [P, NS])
        expert_w = sb("expert_w", [P, NS], I32)
        expert_i = sb("expert_i", [P, NS], I32)
        w_pair = sb("w_pair", [P, TOPK, NT, E])
        w_all = sb("w_all", [P, NT, E])
        w_allT = sb("w_allT", [P, P])
        slot = sb("slot", [P, NT, E])
        picked = sb("picked", [P, TOPK, NT, E])
        pos_i = sb("pos_i", [P, TOPK * NT], I32)
        hi_i = sb("hi_i", [P, TOPK * NT], I32)
        lo_i = sb("lo_i", [P, TOPK * NT], I32)
        hi_f = sb("hi_f", [P, TOPK * NT])
        lo_f = sb("lo_f", [P, TOPK * NT])
        lo_hot = sb("lo_hot", [P, TOPK * NT, P], BF16)
        hi_hot = sb("hi_hot", [P, TOPK * NT, NS], BF16)
        hi_val = sb("hi_val", [P, TOPK * NT, 2, NS], BF16)
        back = sb("back", [P, 2 * NS])
        row_f = sb("row_f", [P, NS])
        empty = sb("empty", [P, NS])
        dst_row = sb("dst_row", [P, NS], I32)
        src_row = sb("src_row", [P, NS], I32)
        top = sb("top", [P, TOPK, NT])
        gap = sb("gap", [P, NT])
        gap_exp = sb("gap_exp", [P, NT])
        gap_den = sb("gap_den", [P, NT])
        half_w = sb("half_w", [P, TOPK, NT])

        xg = sb("xg", [P, RING, P])
        xgT = sb("xgT", [P, RING, P])
        h_pre = sb("h_pre", [P, RING, DF])
        h_act = sb("h_act", [P, RING, DF])
        y_tile = sb("y_tile", [P, RING, P])
        y_back = sb("y_back", [P, TOPK, NT, P])

        xa = sb("xa", [P, 2, P])
        xaT = sb("xaT", [P, 2, P])
        neg = sb("neg", [P, 2, 2 * P])
        expo = sb("expo", [P, 2, 2 * P])
        qk = sb("qk", [P, 2, 2 * P])
        vx = sb("vx", [P, 2, H, VE])
        qT = sb("qT", [P, 2, P])
        kv = sb("kv", [P, 2, H * DH * VE])
        state = sb("state", [P, H * VE])
        prod = sb("prod", [P, H * DH * VE])
        local = sb("local", [P, H, VE])
        nd = sb("nd", [P, H, VE])
        den = sb("den", [P, H])
        rden = sb("rden", [P, H])
        merged = sb("merged", [P, 2, P])
        mT = sb("mT", [P, 2, P])

        xn_rows = [nc.dram_tensor(f"xn_rows{f}", [T, D], F32).ap() for f in range(2)]
        y_rows = [nc.dram_tensor(f"y_rows{f}", [TOPK * T, D], F32).ap() for f in range(2)]

        x_in = [sem(f"x_in{c}") for c in range(NC)]
        wg_in, w2_in, b2_in, attn_in = map(sem, ("wg_in", "w2_in", "b2_in", "attn_in"))
        w1b_in = [sem(f"w1b_in{r}") for r in range(RING)]
        experts_ready = sem("experts_ready")
        b2_blk_ready, w_all_ready, w_allT_ps, w_allT_sb = map(sem, ("b2_blk_ready", "w_all_ready", "w_allT_ps", "w_allT_sb"))
        b2_ps, b2_added = sem("b2_ps"), sem("b2_added")
        const_step, consts = sem("const_step"), sem("consts")
        attn_w_ps, attn_w_sb = sem("attn_w_ps"), sem("attn_w_sb")
        dve_step = sem("dve_step")
        var_ready, std_ready = sem("var_ready"), sem("std_ready")
        xn_ready, xn_stored = sem("xn_ready"), sem("xn_stored")
        xnT_ps, xnT_sb, logits_ps = sem("xnT_ps"), sem("xnT_sb"), sem("logits_ps")
        chosen_ready, counts_ps = sem("chosen_ready"), sem("counts_ps")
        hot_ready, back_ps, table_ready = sem("hot_ready"), sem("back_ps"), sem("table_ready")
        gap_ready, gap_exp_ready = sem("gap_ready"), sem("gap_exp_ready")
        gathered = [sem(f"gathered{r}") for r in range(RING)]
        scattered = [sem(f"scattered{r}") for r in range(RING)]
        xg_ps, xg_sb, h_ps, h_biased, h_gelu = map(sem, ("xg_ps", "xg_sb", "h_ps", "h_biased", "h_gelu"))
        y_ps, y_sb = map(sem, ("y_ps", "y_sb"))
        y_loaded = [sem(f"y_loaded{c}") for c in range(NC)]
        xa_sb, xa_ps, xaT_sb, qkv_ps = map(sem, ("xa_sb", "xa_ps", "xaT_sb", "qkv_ps"))
        neg_sb, exp_sb, v_sb, phi_sb = map(sem, ("neg_sb", "exp_sb", "v_sb", "phi_sb"))
        qT_ps, qT_sb, kv_sb, prefix_ps = map(sem, ("qT_ps", "qT_sb", "kv_sb", "prefix_ps"))
        state_ps, state_sb = map(sem, ("state_ps", "state_sb"))
        prod_sb, local_sb, nd_sb, den_sb, rden_sb = map(sem, ("prod_sb", "local_sb", "nd_sb", "den_sb", "rden_sb"))
        merged_sb, m_ps, mT_sb, proj_ps, x_attn = map(sem, ("merged_sb", "m_ps", "mT_sb", "proj_ps", "x_attn"))
        x_final, out_stored = sem("x_final"), sem("out_stored")

        xg_bank = banks[:, 0, 0:P]
        def y_bank(r): return banks[:, 5 + r, 0:P]
        def h_bank(r): return banks[:, 2 + r, :]
        w_allT_bank = banks[:, 1, 0:P]
        def xnT_bank(c): return banks[:, 2 + c, :]
        logit_bank = banks[:, 6, 0:NT * E]
        before_bank = banks[:, 7, 0:NT * E]
        count_bank = banks[:, 1, 0:E]
        back_bank = banks[:, 0, 0:2 * NS]
        prefix_bank = banks[:, 0:4, 0:H // 4 * DH * VE]
        qkv_bank = banks[:, 4, 0:QD]
        xa_bank, qT_bank, m_bank = (banks[:, 5, k * P:(k + 1) * P] for k in range(3))
        inter_bank = banks[:, 3, H // 4 * DH * VE:H // 4 * DH * VE + H * VE]
        proj_bank = banks[:, 6, 0:P]
        state_bank = banks[:, 7, 0:H * VE]

        def slots(eng, body):
            for r in range(RING):
                body(r, r)
            with eng.Fori(1, NS // RING - 1) as j:
                for r in range(RING):
                    body(j * RING + r, r)
            for r in range(RING):
                body(NS - RING + r, r)

        def tokens(eng, body):
            for i in range(2):
                body(i, i)
            with eng.Fori(1, NT // 2 - 1) as j:
                for r in range(2):
                    body(j * 2 + r, r)
            for i in (NT - 2, NT - 1):
                body(i, i % 2)

        block = ctx.enter_context(nc.Block())

        @block.sync
        def _(sp):
            x_v = x_d[0].rearrange("(t p) d -> p t d", p=P)
            for c in range(NC):
                sp.dma_start(x[:, c * CH:(c + 1) * CH, :], x_v[:, c * CH:(c + 1) * CH, :]).then_inc(x_in[c], 16)
            sp.dma_start(wg[:, :], Wg).then_inc(wg_in, 16)
            sp.dma_start(w2[:, :].rearrange("p (e n) -> p e n", n=P),
                         W2.rearrange("e (c p) d -> p (e c) d", p=P)).then_inc(w2_in, 16)
            for t in range(NT):
                sp.dma_start(b2_rep[t * E:(t + 1) * E, :], b2).then_inc(b2_in, 16)
            for k, w in enumerate((Wq, Wk, Wv, Wo)):
                sp.dma_start(w_raw[:, k, :], w).then_inc(attn_in, 16)
            for k, b in enumerate((bq, bk, bv)):
                sp.dma_start(b_qkv[0:1, k * P:(k + 1) * P], b.rearrange("(a d) -> a d", a=1)).then_inc(attn_in, 16)
            sp.dma_start(b_out[:, :], bo.rearrange("(a d) -> a d", a=1)).then_inc(attn_in, 16)
            for f in range(2):
                rows = xn_rows[f].rearrange("(t p) d -> p t d", p=P)
                for c in range(NC):
                    sp.wait_ge(xn_ready, NT * f + CH * (c + 1))
                    sp.dma_start(rows[:, c * CH:(c + 1) * CH, :], xn[:, c * CH:(c + 1) * CH, :]).then_inc(xn_stored, 16)
                sp.wait_ge(experts_ready, f + 1)
                base = NS * f

                def stage(i, r):
                    e = sp.value_load(expert_i[0:1, bass.ds(i, 1)], min_val=0, max_val=E - 1)
                    at_least(sp, h_ps, base + i - RING + 1)
                    at_least(sp, h_biased, base + i - RING + 1)
                    sp.dma_start(w1b[:, r, :], W1b[bass.ds(e, 1), :, :].rearrange("a p n -> (a p) n")).then_inc(w1b_in[r], 16)

                slots(sp, stage)
                for r in range(RING):
                    sp.wait_ge(scattered[r], 16 * (NS // RING) * (f + 1))
                back_rows = y_rows[f].rearrange("(k t p) d -> k p t d", k=TOPK, p=P)
                for c in range(NC):
                    for k in range(TOPK):
                        sp.dma_start(y_back[:, k, c * CH:(c + 1) * CH, :],
                                     back_rows[k, :, c * CH:(c + 1) * CH, :]).then_inc(y_loaded[c], 16)
            out_v = out_d[0].rearrange("(t p) d -> p t d", p=P)
            for c in range(NC):
                sp.wait_ge(x_final, CH * (c + 1))
                sp.dma_start(out_v[:, c * CH:(c + 1) * CH, :], x[:, c * CH:(c + 1) * CH, :]).then_inc(out_stored, 16)
            sp.wait_ge(out_stored, 16 * NC)

        @block.gpsimd
        def _(pool):
            g = nc.gpsimd
            g.memset(ident[:, :], 0.0).then_inc(const_step, 1)
            g.memset(tri[:, :], 1.0).then_inc(const_step, 1)
            g.memset(strict_bf[:, :], 1.0).then_inc(const_step, 1)
            g.memset(before[:, :, :], 1.0).then_inc(const_step, 1)
            g.memset(head_mask[:, :, :], 1.0).then_inc(const_step, 1)
            pool.wait_ge(const_step, 5)
            g.affine_select(out=ident[:, :], in_=ident[:, :], compare_op=ALU.not_equal, fill=1.0, base=0,
                            pattern=[[-1, P]], channel_multiplier=1).then_inc(consts, 1)
            g.memset(ones_bf[:, :], 1.0).then_inc(consts, 1)
            g.memset(ones_row[:, :], 1.0).then_inc(consts, 1)
            g.affine_select(out=before[:, :, :], in_=before[:, :, :], compare_op=ALU.is_ge, fill=0.0, base=-1,
                            pattern=[[1, E], [-1, E]], channel_multiplier=0).then_inc(consts, 1)
            g.affine_select(out=strict_bf[:, :], in_=strict_bf[:, :], compare_op=ALU.is_ge, fill=0.0, base=-1,
                            pattern=[[1, P]], channel_multiplier=-1).then_inc(consts, 1)
            flt = dict(allow_small_or_imprecise_dtypes=True)
            g.iota(slot_no[:, :], pattern=[[1, NS]], base=0, channel_multiplier=0, **flt).then_inc(consts, 1)
            g.iota(lane_no[:, :], pattern=[[1, P]], base=0, channel_multiplier=0, **flt).then_inc(consts, 1)
            g.iota(full_tiles[:, :], pattern=[[P, NT]], base=0, channel_multiplier=0, **flt).then_inc(consts, 1)
            g.iota(pair_no[:, :], pattern=[[1, TOPK * NT]], base=1, channel_multiplier=0, **flt).then_inc(consts, 1)
            g.iota(own_lane[:, :], pattern=[[0, 1]], base=0, channel_multiplier=1, **flt).then_inc(consts, 1)
            g.affine_select(out=tri[:, :], in_=tri[:, :], compare_op=ALU.is_ge, fill=0.0, base=0,
                            pattern=[[1, P]], channel_multiplier=-1).then_inc(consts, 1)
            g.affine_select(out=head_mask[:, :, :], in_=head_mask[:, :, :], compare_op=ALU.is_ge, fill=0.0, base=0,
                            pattern=[[-DH, H], [0, VE]], channel_multiplier=1).then_inc(const_step, 1)
            pool.wait_ge(const_step, 6)
            g.affine_select(out=head_mask[:, :, :], in_=head_mask[:, :, :], compare_op=ALU.is_ge, fill=0.0,
                            base=DH - 1, pattern=[[DH, H], [0, VE]], channel_multiplier=-1).then_inc(consts, 1)
            g.memset(tile_mask[:, :], 1.0).then_inc(const_step, 1)
            pool.wait_ge(const_step, 7)
            g.affine_select(out=tile_mask[:, :], in_=tile_mask[:, :], compare_op=ALU.is_ge, fill=0.0, base=0,
                            pattern=[[-E, NT]], channel_multiplier=1).then_inc(const_step, 1)
            pool.wait_ge(const_step, 8)
            g.affine_select(out=tile_mask[:, :], in_=tile_mask[:, :], compare_op=ALU.is_ge, fill=0.0, base=E - 1,
                            pattern=[[E, NT]], channel_multiplier=-1).then_inc(const_step, 1)
            pool.wait_ge(const_step, 9)
            pool.wait_ge(b2_in, 16 * NT)
            g.tensor_tensor(b2_blk[:, :, :], b2_rep[:, :].unsqueeze(1).to_broadcast([P, NT, P]),
                            tile_mask[:, :].unsqueeze(2).to_broadcast([P, NT, P]), ALU.mult).then_inc(b2_blk_ready, 1)
            g.memset(vx[:, :, :, :], 1.0).then_inc(consts, 1)
            g.memset(state[:, :], 0.0).then_inc(consts, 1)

            def ffn_moves(f):
                pool.wait_ge(xn_stored, 16 * NC * (f + 1))
                pool.wait_ge(table_ready, f + 1)
                lag = 7
                for n in range(NS + lag):
                    if n < NS:
                        at_least(pool, xg_ps, NS * f + n - RING + 1)
                        g.indirect_dma_start(
                            out=xg[:, n % RING, :], out_offset=None, in_=xn_rows[f][:, :],
                            in_offset=bass.IndirectOffsetOnAxis(ap=src_row[:, n:n + 1], axis=0),
                        ).then_inc(gathered[n % RING], 16)
                    i = n - lag
                    if i >= 0:
                        pool.wait_ge(y_sb, NS * f + i + 1)
                        g.indirect_dma_start(
                            out=y_rows[f][:, :],
                            out_offset=bass.IndirectOffsetOnAxis(ap=dst_row[:, i:i + 1], axis=0),
                            in_=y_tile[:, i % RING, :], in_offset=None,
                            bounds_check=TOPK * T - 1, oob_is_err=False,
                        ).then_inc(scattered[i % RING], 16)

            ffn_moves(0)

            def outer(i, r):
                pool.wait_ge(phi_sb, i + 1)
                pool.wait_ge(v_sb, i + 1)
                at_least(pool, prefix_ps, i - 1)
                k4 = qk[:, r, P:2 * P].rearrange("p (h d) -> p h d", h=H).unsqueeze(3).to_broadcast([P, H, DH, VE])
                v4 = vx[:, r, :, :].unsqueeze(2).to_broadcast([P, H, DH, VE])
                o4 = kv[:, r, :].rearrange("p (h d e) -> p h d e", h=H, d=DH)
                g.tensor_tensor(o4, k4, v4, ALU.mult).then_inc(kv_sb, 1)

            tokens(pool, outer)
            ffn_moves(1)

        @block.scalar
        def _(act):
            s = nc.scalar

            def ln_std(k):
                act.wait_ge(var_ready, k + 1)
                s.activation(std[:, :], var[:, :], ACT.Sqrt).then_inc(std_ready, 1)

            def ffn(f):
                ln_std(2 * f)
                for c in range(NC):
                    act.wait_ge(xnT_ps, NC * f + c + 1)
                    s.copy(xnT[:, c * CH * P:(c + 1) * CH * P], xnT_bank(c)).then_inc(xnT_sb, 1)
                act.wait_ge(gap_ready, f + 1)
                s.activation(gap_exp[:, :], gap[:, :], ACT.Exp).then_inc(gap_exp_ready, 1)
                base = NS * f

                act.wait_ge(w_allT_ps, f + 1)
                s.copy(w_allT[:, :], w_allT_bank).then_inc(w_allT_sb, 1)

                def rows(i, r):
                    act.wait_ge(xg_ps, base + i + 1)
                    at_least(act, h_ps, base + i - RING + 1)
                    s.copy(xgT[:, r, :], xg_bank).then_inc(xg_sb, 1)

                def step(i, r, lead=True):
                    if lead:
                        rows(i + 2, (r + 2) % RING)
                    act.wait_ge(h_biased, base + i + 1)
                    at_least(act, y_ps, base + i - RING + 1)
                    s.activation(h_act[:, r, :], h_pre[:, r, :], ACT.Gelu_apprx_tanh).then_inc(h_gelu, 1)

                rows(0, 0)
                rows(1, 1)
                for r in range(RING):
                    step(r, r)
                with act.Fori(1, NS // RING - 1) as j:
                    for r in range(RING):
                        step(j * RING + r, r)
                for r in range(RING):
                    step(NS - RING + r, r, lead=(r + 2 < RING))

            act.wait_ge(attn_w_ps, 1)
            s.copy(w_attn[:, :, :].rearrange("p k n -> p (k n)"), banks[:, 5, :]).then_inc(attn_w_sb, 1)
            ffn(0)
            ln_std(1)

            def pre(i, r):
                act.wait_ge(xa_ps, i + 1)
                at_least(act, qkv_ps, i - 1)
                s.copy(xaT[:, r, :], xa_bank).then_inc(xaT_sb, 1)
                act.wait_ge(qkv_ps, i + 1)
                at_least(act, exp_sb, i - 1)
                s.activation(neg[:, r, :], qkv_bank[:, 0:2 * P], ACT.Relu, scale=-1.0).then_inc(neg_sb, 1)
                at_least(act, kv_sb, i - 1)
                at_least(act, state_ps, i - 1)
                s.copy(vx[:, r, :, 0:DH], qkv_bank[:, 2 * P:QD].rearrange("p (h d) -> p h d", h=H)).then_inc(v_sb, 1)
                act.wait_ge(neg_sb, i + 1)
                at_least(act, phi_sb, i - 1)
                s.activation(expo[:, r, :], neg[:, r, :], ACT.Exp, scale=-1.0).then_inc(exp_sb, 1)

            def post(i, r):
                act.wait_ge(m_ps, i + 1)
                at_least(act, proj_ps, i - 1)
                s.copy(mT[:, r, :], m_bank).then_inc(mT_sb, 1)

            act.wait_ge(consts, 14)
            pre(0, 0)
            pre(1, 1)

            def attn(i, r, lead=True):
                act.wait_ge(qT_ps, i + 1)
                at_least(act, prefix_ps, i - 1)
                s.copy(qT[:, r, :], qT_bank).then_inc(qT_sb, 1)
                if lead:
                    pre(i + 2, r)
                if not (isinstance(i, int) and i == 0):
                    post(i - 1, 1 - r)

            for i in range(2):
                attn(i, i)
            with act.Fori(1, NT // 2 - 1) as j:
                for r in range(2):
                    attn(2 * j + r, r)
            for i in (NT - 2, NT - 1):
                attn(i, i % 2, lead=False)
            post(NT - 1, (NT - 1) % 2)
            ffn(1)

        @block.vector
        def _(dve):
            v = nc.vector
            steps = [0]

            def link(ins):
                steps[0] += 1
                ins.then_inc(dve_step, 1)
                dve.wait_ge(dve_step, steps[0])

            def ln_moments(k):
                me, mo = stats[:, :, 1], stats[:, :, 4]
                v.tensor_tensor(m_sum[:, :], me, mo, ALU.add).then_inc(dve_step, 1)
                v.tensor_tensor(v_sum[:, :], stats[:, :, 2], stats[:, :, 5], ALU.add).then_inc(dve_step, 1)
                steps[0] += 2
                link(v.tensor_tensor(m_dif[:, :], me, mo, ALU.subtract))
                v.tensor_scalar(mean[:, :], m_sum[:, :], 0.5, None, ALU.mult).then_inc(dve_step, 1)
                steps[0] += 1
                link(v.scalar_tensor_tensor(out=v_dif[:, :], in0=m_dif[:, :], scalar=0.25, in1=m_dif[:, :],
                                            op0=ALU.mult, op1=ALU.mult))
                link(v.scalar_tensor_tensor(out=v_dif[:, :], in0=v_sum[:, :], scalar=1.0 / D, in1=v_dif[:, :],
                                            op0=ALU.mult, op1=ALU.add))
                v.tensor_scalar(var[:, :], v_dif[:, :], LN_EPS, None, ALU.add).then_inc(var_ready, 1)
                dve.wait_ge(std_ready, k + 1)
                link(v.reciprocal(rstd[:, :], std[:, :]))

            def gate_and_route(f):
                for t in range(NT):
                    v.tensor_scalar(xn[:, t, :], x[:, t, :], mean[:, t:t + 1], rstd[:, t:t + 1],
                                    ALU.subtract, ALU.mult).then_inc(xn_ready, 1)
                dve.wait_ge(logits_ps, f + 1)
                link(v.tensor_copy(logit[:, :, :].rearrange("p t e -> p (t e)"), logit_bank))
                if f == 0:
                    dve.wait_ge(consts, 14)
                mine = logit[:, :, :].unsqueeze(3).to_broadcast([P, NT, E, E])
                other = logit[:, :, :].unsqueeze(2).to_broadcast([P, NT, E, E])
                v.tensor_tensor(beats[:, :, :, :], other, mine, ALU.is_gt).then_inc(dve_step, 1)
                steps[0] += 1
                link(v.tensor_tensor(ties[:, :, :, :], other, mine, ALU.is_equal))
                link(v.tensor_tensor(ties[:, :, :, :], ties[:, :, :, :],
                                     before[:, :, :].unsqueeze(1).to_broadcast([P, NT, E, E]), ALU.mult))
                link(v.tensor_tensor(beats[:, :, :, :], beats[:, :, :, :], ties[:, :, :, :], ALU.add))
                link(v.tensor_reduce(rank[:, :, :], beats[:, :, :, :], AX.X, ALU.add))
                v.tensor_scalar(chosen[:, :, :], rank[:, :, :], float(TOPK), None, ALU.is_lt).then_inc(chosen_ready, 1)
                v.tensor_scalar(is_rank[:, 0, :, :], rank[:, :, :], 0.0, None, ALU.is_equal).then_inc(dve_step, 1)
                steps[0] += 1
                link(v.tensor_scalar(is_rank[:, 1, :, :], rank[:, :, :], 1.0, None, ALU.is_equal))
                both = logit[:, :, :].unsqueeze(1).to_broadcast([P, TOPK, NT, E])
                link(v.tensor_tensor(picked[:, :, :, :], is_rank[:, :, :, :], both, ALU.mult))
                link(v.tensor_reduce(top[:, :, :], picked[:, :, :, :], AX.X, ALU.add))
                v.tensor_tensor(gap[:, :], top[:, 1, :], top[:, 0, :], ALU.subtract).then_inc(gap_ready, 1)
                dve.wait_ge(counts_ps, f + 1)
                link(v.tensor_copy(tiles_of[:, :], count_bank))
                link(v.tensor_tensor(more[:, :, :], tiles_of[:, :].unsqueeze(2).to_broadcast([P, E, NT]),
                                     full_tiles[:, :].unsqueeze(1).to_broadcast([P, E, NT]), ALU.is_gt))
                link(v.tensor_reduce(tiles_of[:, :], more[:, :, :], AX.X, ALU.add))
                link(v.tensor_tensor(below[:, :, :], before[:, :, :],
                                     tiles_of[:, :].unsqueeze(1).to_broadcast([P, E, E]), ALU.mult))
                link(v.tensor_reduce(first_tile[:, :], below[:, :, :], AX.X, ALU.add))
                v.tensor_tensor(end_tile[:, :], first_tile[:, :], tiles_of[:, :], ALU.add).then_inc(dve_step, 1)
                steps[0] += 1
                link(v.tensor_scalar(first_tile[:, :], first_tile[:, :], float(P), None, ALU.mult))
                link(v.tensor_tensor(slot[:, :, :], before_bank.rearrange("p (t e) -> p t e", e=E),
                                     first_tile[:, :].unsqueeze(1).to_broadcast([P, NT, E]), ALU.add))
                link(v.tensor_tensor(picked[:, :, :, :], is_rank[:, :, :, :],
                                     slot[:, :, :].unsqueeze(1).to_broadcast([P, TOPK, NT, E]), ALU.mult))
                with nc.allow_low_precision(reason="whole numbers below 2 ** 24, summed in float32"):
                    link(v.tensor_reduce(pos_i[:, :], picked[:, :, :, :].rearrange("p k t e -> p (k t) e"),
                                         AX.X, ALU.add))
                v.tensor_scalar(hi_i[:, :], pos_i[:, :], 7, None, ALU.logical_shift_right).then_inc(dve_step, 1)
                steps[0] += 1
                link(v.tensor_scalar(lo_i[:, :], pos_i[:, :], P - 1, None, ALU.bitwise_and))
                v.tensor_copy(hi_f[:, :], hi_i[:, :]).then_inc(dve_step, 1)
                steps[0] += 1
                link(v.tensor_copy(lo_f[:, :], lo_i[:, :]))
                KT = TOPK * NT
                link(v.tensor_tensor(hi_hot[:, :, :], slot_no[:, :].unsqueeze(1).to_broadcast([P, KT, NS]),
                                     hi_f[:, :].unsqueeze(2).to_broadcast([P, KT, NS]), ALU.is_equal))
                v.tensor_scalar(hi_val[:, :, 0, :], hi_hot[:, :, :], own_lane[:, 0:1], None,
                                ALU.mult).then_inc(hot_ready, 1)
                v.tensor_tensor(hi_val[:, :, 1, :], hi_hot[:, :, :],
                                pair_no[:, :].unsqueeze(2).to_broadcast([P, KT, NS]), ALU.mult).then_inc(hot_ready, 1)
                for q in range(KT):
                    v.tensor_scalar(lo_hot[:, q, :], lane_no[:, :], lo_f[:, q:q + 1], None,
                                    ALU.is_equal).then_inc(hot_ready, 1)
                link(v.tensor_tensor(past[:, :, :], slot_no[:, :].unsqueeze(2).to_broadcast([P, NS, E]),
                                     end_tile[:, :].unsqueeze(1).to_broadcast([P, NS, E]), ALU.is_ge))
                link(v.tensor_reduce(expert_f[:, :], past[:, :, :], AX.X, ALU.add))
                v.tensor_scalar(expert_w[:, :], expert_f[:, :], float(E - 1), float(DF), ALU.min, ALU.mult).then_inc(dve_step, 1)
                steps[0] += 1
                v.tensor_scalar(expert_i[:, :], expert_f[:, :], float(E - 1), None, ALU.min).then_inc(experts_ready, 1)
                dve.wait_ge(back_ps, f + 1)
                link(v.tensor_copy(back[:, :], back_bank))
                v.tensor_scalar(empty[:, :], back[:, NS:2 * NS], 0.0, float(PAD), ALU.is_equal, ALU.mult).then_inc(dve_step, 1)
                steps[0] += 1
                link(v.scalar_tensor_tensor(out=row_f[:, :], in0=back[:, NS:2 * NS], scalar=float(P), in1=back[:, 0:NS],
                                            op0=ALU.mult, op1=ALU.add))
                link(v.scalar_tensor_tensor(out=dst_row[:, :], in0=row_f[:, :], scalar=-float(P), in1=empty[:, :],
                                            op0=ALU.add, op1=ALU.add))
                v.tensor_scalar(src_row[:, :], dst_row[:, :], T - 1, None, ALU.bitwise_and).then_inc(table_ready, 1)
                dve.wait_ge(gap_exp_ready, f + 1)
                link(v.tensor_scalar(gap_den[:, :], gap_exp[:, :], 1.0, 2.0, ALU.add, ALU.mult))
                link(v.reciprocal(half_w[:, 0, :], gap_den[:, :]))
                link(v.tensor_tensor(half_w[:, 1, :], half_w[:, 0, :], gap_exp[:, :], ALU.mult))
                link(v.tensor_tensor(w_pair[:, :, :, :], is_rank[:, :, :, :],
                                     half_w[:, :, :].unsqueeze(3).to_broadcast([P, TOPK, NT, E]), ALU.mult))
                v.tensor_tensor(w_all[:, :, :], w_pair[:, 0, :, :], w_pair[:, 1, :, :], ALU.add).then_inc(w_all_ready, 1)

            def experts(f):
                base = NS * f
                dve.wait_ge(b2_ps, f + 1)
                for t in range(NT):
                    v.tensor_tensor(x[:, t, :], banks[:, 2 + t // CH, (t % CH) * P:(t % CH + 1) * P], x[:, t, :],
                                    ALU.add).then_inc(b2_added, 1)

                def hidden(i, r):
                    dve.wait_ge(h_ps, base + i + 1)
                    at_least(dve, h_gelu, base + i - RING + 1)
                    v.tensor_tensor(h_pre[:, r, :].rearrange("p (c n) -> p c n", c=FC),
                                    h_bank(r).rearrange("p (c n) -> p c n", c=FC),
                                    w1b[:, r, DF:DF + FC].unsqueeze(2).to_broadcast([P, FC, P]),
                                    ALU.add).then_inc(h_biased, 1)

                def output(j, r):
                    i = j * RING + r
                    dve.wait_ge(y_ps, base + i + 1)
                    at_least(dve, scattered[r], j * 16 + 16 * (NS // RING) * f)
                    v.tensor_copy(y_tile[:, r, :], y_bank(r)).then_inc(y_sb, 1)

                LAG = 2
                hidden(0, 0)
                hidden(1, 1)
                hidden(2, 2)
                output(0, 0)
                with dve.Fori(1, NS // RING) as j:
                    for r in range(RING):
                        hidden(j * RING + r, r)
                        output(j if r >= LAG else j - 1, (r - LAG) % RING)
                output(NS // RING - 1, RING - 2)
                output(NS // RING - 1, RING - 1)

            def combine(f):
                for t in range(NT):
                    if t % CH == 0:
                        dve.wait_ge(y_loaded[t // CH], 16 * TOPK * (f + 1))
                    v.scalar_tensor_tensor(out=y_back[:, 0, t, :], in0=y_back[:, 0, t, :],
                                           scalar=half_w[:, 0, t:t + 1], in1=x[:, t, :],
                                           op0=ALU.mult, op1=ALU.add).then_inc(dve_step, 1)
                first = steps[0]
                steps[0] += NT
                for t in range(NT):
                    dve.wait_ge(dve_step, first + t + 1)
                    v.scalar_tensor_tensor(out=x[:, t, :], in0=y_back[:, 1, t, :],
                                           scalar=half_w[:, 1, t:t + 1], in1=y_back[:, 0, t, :],
                                           op0=ALU.mult, op1=ALU.add).then_inc(x_final if f else dve_step, 1)
                if f == 0:
                    second = steps[0]
                    steps[0] += NT
                    for t in range(NT):
                        dve.wait_ge(dve_step, second + t + 1)
                        v.bn_stats(stats[:, t, :], x[:, t, :]).then_inc(dve_step, 1)
                    steps[0] += NT
                    dve.wait_ge(dve_step, steps[0])

            for t in range(NT):
                if t % CH == 0:
                    dve.wait_ge(x_in[t // CH], 16)
                v.bn_stats(stats[:, t, :], x[:, t, :]).then_inc(dve_step, 1)
            steps[0] += NT
            dve.wait_ge(dve_step, steps[0])
            ln_moments(0)
            gate_and_route(0)
            experts(0)
            combine(0)
            ln_moments(1)

            def norm(i, r):
                at_least(dve, xa_ps, i - 1)
                v.tensor_scalar(xa[:, r, :], x[:, bass.ds(i, 1), :].rearrange("p a d -> p (a d)"),
                                mean[:, bass.ds(i, 1)], rstd[:, bass.ds(i, 1)],
                                ALU.subtract, ALU.mult).then_inc(xa_sb, 1)

            def phi(i, r):
                dve.wait_ge(exp_sb, i + 1)
                at_least(dve, local_sb, i - 1)
                at_least(dve, kv_sb, i - 1)
                at_least(dve, state_ps, i - 1)
                v.scalar_tensor_tensor(out=qk[:, r, :], in0=qkv_bank[:, 0:2 * P], scalar=0.0, in1=expo[:, r, :],
                                       op0=ALU.max, op1=ALU.add).then_inc(phi_sb, 1)

            def attend(i, r):
                dve.wait_ge(prefix_ps, i + 1)
                at_least(dve, local_sb, i)
                q4 = qk[:, r, 0:P].rearrange("p (b n) -> p b n", b=4).unsqueeze(3).to_broadcast([P, 4, P // 4, VE])
                v.tensor_tensor(prod[:, :].rearrange("p (b n e) -> p b n e", b=4, e=VE),
                                prefix_bank.rearrange("p b (n e) -> p b n e", e=VE), q4, ALU.mult).then_inc(prod_sb, 1)
                dve.wait_ge(prod_sb, i + 1)
                at_least(dve, nd_sb, i)
                v.tensor_reduce(local[:, :, :], prod[:, :].rearrange("p (h d e) -> p h e d", h=H, d=DH),
                                AX.X, ALU.add).then_inc(local_sb, 1)
                dve.wait_ge(local_sb, i + 1)
                v.tensor_tensor(nd[:, :, :], inter_bank.rearrange("p (h e) -> p h e", h=H), local[:, :, :],
                                ALU.add).then_inc(nd_sb, 1)
                dve.wait_ge(state_ps, i + 1)
                v.tensor_tensor(state[:, :], state_bank, head_mask[:, :, :].rearrange("p h e -> p (h e)"),
                                ALU.mult).then_inc(state_sb, 1)
                dve.wait_ge(nd_sb, i + 1)
                v.tensor_scalar(den[:, :], nd[:, :, DH], ATT_EPS, None, ALU.add).then_inc(den_sb, 1)
                dve.wait_ge(den_sb, i + 1)
                v.reciprocal(rden[:, :], den[:, :]).then_inc(rden_sb, 1)
                dve.wait_ge(rden_sb, i + 1)
                at_least(dve, m_ps, i - 1)
                v.tensor_tensor(merged[:, r, :].rearrange("p (h d) -> p h d", h=H), nd[:, :, 0:DH],
                                rden[:, :].unsqueeze(2).to_broadcast([P, H, DH]), ALU.mult).then_inc(merged_sb, 1)

            def residual(i):
                dve.wait_ge(proj_ps, i + 1)
                xt = x[:, bass.ds(i, 1), :].rearrange("p a d -> p (a d)")
                v.tensor_tensor(xt, proj_bank, xt, ALU.add).then_inc(x_attn, 1)

            norm(0, 0)
            norm(1, 1)
            phi(0, 0)

            def attn(i, r, norms=True, phis=True):
                if norms:
                    norm(i + 2, r)
                if phis:
                    phi(i + 1, 1 - r)
                attend(i, r)
                if not (isinstance(i, int) and i == 0):
                    residual(i - 1)

            for i in range(2):
                attn(i, i)
            with dve.Fori(1, NT // 2 - 1) as j:
                for r in range(2):
                    attn(2 * j + r, r)
            attn(NT - 2, 0, norms=False)
            attn(NT - 1, 1, norms=False, phis=False)
            residual(NT - 1)

            dve.wait_ge(x_attn, NT)
            for t in range(NT):
                v.bn_stats(stats[:, t, :], x[:, t, :]).then_inc(dve_step, 1)
            steps[0] += NT
            dve.wait_ge(dve_step, steps[0])
            ln_moments(2)
            gate_and_route(1)
            experts(1)
            combine(1)

        @block.tensor
        def _(pe):
            mm = nc.tensor.matmul
            pe.wait_ge(consts, 14)

            def gate(f):
                for c in range(NC):
                    for t in range(c * CH, (c + 1) * CH):
                        pe.wait_ge(xn_ready, NT * f + t + 1)
                        last = pe.transpose(xnT_bank(c)[:, (t % CH) * P:(t % CH + 1) * P], xn[:, t, :], ident[:, :])
                    last.then_inc(xnT_ps, 1)
                if f == 0:
                    pe.wait_ge(wg_in, 16)
                for t in range(NT):
                    pe.wait_ge(xnT_sb, NC * f + t // CH + 1)
                    last = mm(logit_bank[:, t * E:(t + 1) * E], xnT[:, t * P:(t + 1) * P], wg[:, :],
                              start=True, stop=True)
                last.then_inc(logits_ps, 1)

            def route(f):
                pe.wait_ge(chosen_ready, f + 1)
                for t in range(NT):
                    mm(count_bank, ones_bf[:, :], chosen[:, t, :], start=(t == 0), stop=(t == NT - 1))
                for t in range(NT - 1):
                    left = NT - 1 - t
                    mm(before_bank[:, (t + 1) * E:], ones_bf[:, :],
                       chosen[:, t, :].unsqueeze(1).to_broadcast([P, left, E]), start=(t == 0),
                       stop=False, skip_group_check=True)
                last = mm(before_bank, strict_bf[:, :], chosen[:, :, :].rearrange("p t e -> p (t e)"),
                          start=False, stop=True, skip_group_check=True)
                last.then_inc(counts_ps, 1)
                KT = TOPK * NT
                for q in range(KT):
                    pe.wait_ge(hot_ready, (KT + 2) * f + 2 + q + 1)
                    last = mm(back_bank, lo_hot[:, q, :], hi_val[:, q, :, :].rearrange("p a s -> p (a s)"),
                              start=(q == 0), stop=(q == KT - 1))
                last.then_inc(back_ps, 1)

            def experts(f):
                base = NS * f
                pe.wait_ge(table_ready, f + 1)
                if f == 0:
                    pe.wait_ge(w2_in, 16)
                    pe.wait_ge(b2_blk_ready, 1)
                pe.wait_ge(w_all_ready, f + 1)
                pe.transpose(w_allT_bank, w_all[:, :, :].rearrange("p t e -> p (t e)"), ident[:, :]).then_inc(w_allT_ps, 1)
                pe.wait_ge(w_allT_sb, f + 1)
                for c in range(NC):
                    last = mm(banks[:, 2 + c, :], w_allT[:, :],
                              b2_blk[:, c * CH:(c + 1) * CH, :].rearrange("p t n -> p (t n)"), start=True, stop=True)
                last.then_inc(b2_ps, 1)

                def hidden(j, r, ahead):
                    i = j * RING + r + ahead
                    q = (r + ahead) % RING
                    fills = j + (r + ahead) // RING + 1
                    pe.wait_ge(w1b_in[q], fills * 16 + 16 * (NS // RING) * f)
                    pe.wait_ge(xg_sb, base + i + 1)
                    at_least(pe, h_biased, base + i - RING + 1)
                    for c in range(FC):
                        last = mm(h_bank(q)[:, c * P:(c + 1) * P], w1b[:, q, c * P:(c + 1) * P], xgT[:, q, :],
                                  start=True, stop=True)
                    last.then_inc(h_ps, 1)

                def output(i, r):
                    col = pe.value_load(expert_w[0:1, bass.ds(i, 1)], min_val=0, max_val=(E - 1) * DF)
                    pe.wait_ge(h_gelu, base + i + 1)
                    at_least(pe, y_sb, base + i - RING + 1)
                    for c in range(FC):
                        last = mm(y_bank(r), h_act[:, r, c * P:(c + 1) * P], w2[:, bass.ds(col + c * P, P)],
                                  start=(c == 0), stop=(c == FC - 1))
                    last.then_inc(y_ps, 1)

                def transposed_rows(j, r, ahead):
                    slot_r = (r + ahead) % RING
                    fills = j + (r + ahead) // RING + 1
                    pe.wait_ge(gathered[slot_r], fills * 16 + 16 * (NS // RING) * f)
                    at_least(pe, xg_sb, base + j * RING + r + ahead)
                    pe.transpose(xg_bank, xg[:, slot_r, :], ident[:, :]).then_inc(xg_ps, 1)

                def step(j, r, last=False):
                    i = j * RING + r
                    if not (last and r + 2 >= RING):
                        transposed_rows(j, r, 2)
                    if not (last and r + 1 >= RING):
                        hidden(j, r, 1)
                    if not (isinstance(i, int) and i == 0):
                        output(i - 1, (r - 1) % RING)

                transposed_rows(0, 0, 0)
                transposed_rows(0, 1, 0)
                pe.wait_ge(b2_added, NT * (f + 1))
                hidden(0, 0, 0)
                for r in range(RING):
                    step(0, r)
                with pe.Fori(1, NS // RING - 1) as j:
                    for r in range(RING):
                        step(j, r)
                for r in range(RING):
                    step(NS // RING - 1, r, last=True)
                output(NS - 1, (NS - 1) % RING)

            pe.wait_ge(attn_in, 16 * 8)
            for k in range(4):
                last = pe.transpose(banks[:, 5, k * P:(k + 1) * P], w_raw[:, k, :], ident[:, :])
            last.then_inc(attn_w_ps, 1)
            pe.wait_ge(attn_w_sb, 1)
            gate(0)
            route(0)
            experts(0)

            wqkv = w_attn[:, 0:3, :].rearrange("p k n -> p (k n)")

            def project(i, r):
                pe.wait_ge(xa_sb, i + 1)
                at_least(pe, xaT_sb, i)
                at_least(pe, qT_sb, i - 1)
                at_least(pe, mT_sb, i - 3)
                pe.transpose(xa_bank, xa[:, r, :], ident[:, :]).then_inc(xa_ps, 1)
                at_least(pe, phi_sb, i)
                at_least(pe, exp_sb, i)
                mm(qkv_bank, ones_row[:, :], b_qkv[:, :], start=True, stop=False)
                pe.wait_ge(xaT_sb, i + 1)
                mm(qkv_bank, xaT[:, r, :], wqkv, start=False, stop=True).then_inc(qkv_ps, 1)

            def out_proj(i, r, lead=True, last=False):
                pe.wait_ge(merged_sb, i + 1)
                at_least(pe, mT_sb, i)
                pe.wait_ge(qT_sb, i + 2 if not last else NT)
                pe.wait_ge(xaT_sb, i + 4 if lead else NT)
                pe.transpose(m_bank, merged[:, r, :], ident[:, :]).then_inc(m_ps, 1)
                at_least(pe, x_attn, i)
                mm(proj_bank, ones_row[:, :], b_out[:, :], start=True, stop=False)
                pe.wait_ge(mT_sb, i + 1)
                mm(proj_bank, mT[:, r, :], w_attn[:, 3, :], start=False, stop=True).then_inc(proj_ps, 1)

            def attn(i, r, lead=True):
                pe.wait_ge(phi_sb, i + 1)
                pe.wait_ge(xaT_sb, i + 2 if lead else NT)
                at_least(pe, mT_sb, i - 1)
                pe.transpose(qT_bank, qk[:, r, 0:P], ident[:, :]).then_inc(qT_ps, 1)
                pe.wait_ge(kv_sb, i + 1)
                at_least(pe, nd_sb, i)
                n = H // 4 * DH * VE
                for b in range(4):
                    mm(prefix_bank[:, b, :], tri[:, :], kv[:, r, b * n:(b + 1) * n], start=True, stop=True)
                pe.wait_ge(qT_sb, i + 1)
                if not (isinstance(i, int) and i == 0):
                    pe.wait_ge(state_sb, i)
                mm(inter_bank, qT[:, r, :], state[:, :], start=True, stop=True).then_inc(prefix_ps, 1)
                mm(state_bank, qk[:, r, P:2 * P], vx[:, r, :, :].rearrange("p h e -> p (h e)"),
                   start=(isinstance(i, int) and i == 0), stop=True, skip_group_check=True).then_inc(state_ps, 1)
                if lead:
                    project(i + 2, r)
                if not (isinstance(i, int) and i == 0):
                    out_proj(i - 1, 1 - r, lead)

            project(0, 0)
            project(1, 1)
            for i in range(2):
                attn(i, i)
            with pe.Fori(1, NT // 2 - 1) as j:
                for r in range(2):
                    attn(2 * j + r, r)
            for i in (NT - 2, NT - 1):
                attn(i, i % 2, lead=False)
            out_proj(NT - 1, (NT - 1) % 2, lead=False, last=True)
            gate(1)
            route(1)
            experts(1)


_INS = ['L0_attn_x', 'L0_attn_Wq', 'L0_attn_bq', 'L0_attn_Wk', 'L0_attn_bk', 'L0_attn_Wv', 'L0_attn_bv',
        'L0_attn_Wo', 'L0_attn_bo', 'L0_ffn_Wg', 'W1b', 'L0_ffn_W2', 'L0_ffn_b2']


def kernel(**inputs):
    import numpy as _np
    import concourse.bacc as _bacc
    from concourse import mybir as _mybir
    from concourse.bass_utils import run_bass_kernel_spmd as _run

    nc = _bacc.Bacc("TRN2", target_bir_lowering=False, num_devices=1)
    W1, b1 = _np.asarray(inputs['L0_ffn_W1']), _np.asarray(inputs['L0_ffn_b1'])
    E, D, DF = W1.shape
    inputs['W1b'] = _np.concatenate([W1, b1.reshape(E, DF // P, P).transpose(0, 2, 1)], axis=2)
    arrays, args = {}, []
    for name in _INS:
        a = _np.ascontiguousarray(inputs[name])
        arrays[f"in_{name}"] = a
        args.append(nc.dram_tensor(f"in_{name}", a.shape, _mybir.dt.from_np(a.dtype), kind="ExternalInput").ap())
    shape = inputs['L0_attn_x'].shape
    out = nc.dram_tensor("out_0", shape, _mybir.dt.float32, kind="ExternalOutput").ap()
    macaron_kernel(nc, *args, out)
    r = _run(nc, [arrays], core_ids=[0])
    return r.results[0]["out_0"]
```

```python
from contextlib import ExitStack

import concourse.bass as bass
from concourse import mybir

F32 = mybir.dt.float32
F32R = mybir.dt.float32r
BF16 = mybir.dt.bfloat16
I32 = mybir.dt.int32
U32 = mybir.dt.uint32
ALU = mybir.AluOpType
ACT = mybir.ActivationFunctionType
AX = mybir.AxisListType

P = 128
RING = 3


def at_least(eng, sem, value):
    if isinstance(value, int) and value <= 0:
        return
    eng.wait_ge(sem, value)


def macaron_kernel(nc, x_d, Wq, bq, Wk, bk, Wv, bv, Wo, bo, Wg, W1b, W2, b2, out_d):
    T, D = x_d.shape[1], x_d.shape[2]
    E, DF = W2.shape[0], W2.shape[1]
    H, DH = 16, D // 16
    NT = T // P
    FC = DF // P
    TOPK = 2
    NS = (TOPK * T + E * (P - 1)) // P
    QD = 3 * D
    VE = DH + 1
    PAD = 2 * TOPK * T
    LN_EPS, ATT_EPS = 1e-5, 1e-6
    CH = 4
    WARM_COUNTS, WARM_HOTS, WARM_INVERSE, WARM_EXPERTS, WARM_ATTENTION, WARM_PROJECT = 8, 4, 4, 8, 9, 4
    NC = NT // CH
    KT = TOPK * NT
    HOTS = ((0, 8), (8, 16), (16, 20))
    ACT_Q, POOL_Q = 20, 30
    assert D == P and NS % RING == 0 and T & (T - 1) == 0

    with ExitStack() as ctx:
        def sb(name, shape, dt=F32):
            return ctx.enter_context(nc.sbuf_tensor(name, shape, dt))

        def sem(name):
            return ctx.enter_context(nc.semaphore(name))

        banks = ctx.enter_context(nc.psum_tensor("banks", [P, 8, 512], F32))

        ident = sb("ident", [P, P])
        blank = sb("blank", [P, 4 * P], BF16)
        tri = sb("tri", [P, P])
        strict_bf = sb("strict_bf", [P, P], BF16)
        ones_bf = sb("ones_bf", [P, P], BF16)
        ones2 = sb("ones2", [2, P], F32R)
        before = sb("before", [P, E, E])
        head_mask = sb("head_mask", [P, VE, H])
        slot_no = sb("slot_no", [P, NS])
        lane_no = sb("lane_no", [P, P], BF16)
        full_tiles = sb("full_tiles", [P, NT])
        pair_no = sb("pair_no", [P, TOPK * NT])
        own_lane = sb("own_lane", [P, 1])

        w2 = sb("w2", [P, E * DF])
        w1b = sb("w1b", [P, RING, DF + FC])
        b2_rep = sb("b2_rep", [P, P])
        b2_blk = sb("b2_blk", [P, NT, P])
        tile_mask = sb("tile_mask", [P, NT])
        wg = sb("wg", [P, E])
        w_raw = sb("w_raw", [P, 4, P])
        w_attn = sb("w_attn", [P, 4, P])
        bias = sb("bias", [2, QD + P])
        bias_hi = sb("bias_hi", [2, QD + P], F32R)
        bias_lo = sb("bias_lo", [2, QD + P])
        bias_2 = sb("bias_2", [2, QD + P], F32R)
        row_0 = sb("row_0", [2, 1])

        x = sb("x", [P, NT, P])
        xn = sb("xn", [P, NT, P])
        xnT = sb("xnT", [P, NT * P])
        stats = sb("stats", [P, NT, 6])
        m_sum = sb("m_sum", [P, NT])
        m_dif = sb("m_dif", [P, NT])
        v_sum = sb("v_sum", [P, NT])
        v_dif = sb("v_dif", [P, NT])
        mean = sb("mean", [P, NT])
        var = sb("var", [P, NT])
        std = sb("std", [P, NT])
        minus_half = sb("minus_half", [P, NT])
        rstd = sb("rstd", [P, NT])
        shift = sb("shift", [P, NT])
        halves_3 = sb("halves_3", [P, 2, 2])
        apart_3 = sb("apart_3", [P, 2])
        apart_quarter_3 = sb("apart_quarter_3", [P, 2])
        var_3 = sb("var_3", [P, 2])
        halves_scale = sb("halves_scale", [P, 2, 2])
        quarter = sb("quarter", [P, 2])
        eps = sb("eps", [P, 2])
        rstd_3 = sb("rstd_3", [P, NT])
        shift_3 = sb("shift_3", [P, NT])

        logit = sb("logit", [P, NT, E])
        beats = sb("beats", [P, NT, E, E])
        rank = sb("rank", [P, NT, E])
        is_rank = sb("is_rank", [P, TOPK, NT, E])
        chosen = sb("chosen", [P, NT, E], BF16)
        more = sb("more", [P, E, NT])
        tiles_of = sb("tiles_of", [P, E])
        below = sb("below", [P, E, E])
        first_tile = sb("first_tile", [P, E])
        end_tile = sb("end_tile", [P, E])
        past = sb("past", [P, NS, E])
        expert_f = sb("expert_f", [P, NS])
        expert_w = sb("expert_w", [P, NS], I32)
        expert_i = sb("expert_i", [P, NS], I32)
        w_pair = sb("w_pair", [P, TOPK, NT, E])
        w_all = sb("w_all", [P, NT, E])
        w_allT = sb("w_allT", [P, P])
        slot = sb("slot", [P, NT, E])
        picked = sb("picked", [P, TOPK, NT, E])
        pos_i = sb("pos_i", [P, TOPK * NT], I32)
        hi_i = sb("hi_i", [P, TOPK * NT], I32)
        lo_i = sb("lo_i", [P, TOPK * NT], I32)
        hi_f = sb("hi_f", [P, TOPK * NT])
        lo_f = sb("lo_f", [P, TOPK * NT])
        off = sb("off", [P, POOL_Q - ACT_Q, P], BF16)
        warm = sb("warm", [P, 2, 3])
        lo_hot = sb("lo_hot", [P, TOPK * NT, P], BF16)
        hi_hot = sb("hi_hot", [P, TOPK * NT, NS], BF16)
        hi_val = sb("hi_val", [P, TOPK * NT, 2, NS], BF16)
        back = sb("back", [P, 2 * NS])
        row_f = sb("row_f", [P, NS])
        empty = sb("empty", [P, NS])
        dst_row = sb("dst_row", [P, NS], I32)
        src_row = sb("src_row", [P, NS], I32)
        top = sb("top", [P, TOPK, NT])
        gap = sb("gap", [P, NT])
        gap_exp = sb("gap_exp", [P, NT])
        gap_den = sb("gap_den", [P, NT])
        half_w = sb("half_w", [P, TOPK, NT])

        xg = sb("xg", [P, RING, P])
        xgT = sb("xgT", [P, RING, P])
        h_pre = sb("h_pre", [P, RING, DF])
        h_act = sb("h_act", [P, RING, DF])
        y_tile = sb("y_tile", [P, RING, P])
        y_back = sb("y_back", [P, TOPK, NT, P])

        xn_ring = sb("xn_ring", [P, 2, P])
        xa = sb("xa", [P, 2, P])
        xaT = sb("xaT", [P, 2, P])
        neg = sb("neg", [P, 2, 2 * P])
        expo = sb("expo", [P, 2, 2 * P])
        qk = sb("qk", [P, 2, 2 * P])
        vx = sb("vx", [P, 2, VE, H])
        qT = sb("qT", [P, 2, P])
        kv = sb("kv", [P, 2, DH, P])
        state = sb("state", [P, H * VE])
        prod = sb("prod", [P, VE * P])
        local = sb("local", [P, VE, H])
        nd = sb("nd", [P, VE, H])
        den = sb("den", [P, H])
        rden = sb("rden", [P, H])
        merged = sb("merged", [P, 2, P])
        mT = sb("mT", [P, 2, P])

        xn_rows = [nc.dram_tensor(f"xn_rows{f}", [T, D], F32).ap() for f in range(2)]
        y_rows = [nc.dram_tensor(f"y_rows{f}", [TOPK * T, D], F32).ap() for f in range(2)]

        x_in = [sem(f"x_in{c}") for c in range(NC)]
        wg_in, w2_in, b2_in, attn_in = map(sem, ("wg_in", "w2_in", "b2_in", "attn_in"))
        w1b_in = [sem(f"w1b_in{r}") for r in range(RING)]
        experts_ready, expert_w_ready = sem("experts_ready"), sem("expert_w_ready")
        b2_blk_ready, w_all_ready, w_allT_ps, w_allT_sb = map(
            sem, ("b2_blk_ready", "w_all_ready", "w_allT_ps", "w_allT_sb"))
        b2_ps, b2_added, x_mid = sem("b2_ps"), sem("b2_added"), sem("x_mid")
        const_step, consts, blank_ready = sem("const_step"), sem("consts"), sem("blank_ready")
        attn_w_ps, attn_w_sb = sem("attn_w_ps"), sem("attn_w_sb")
        dve_step = sem("dve_step")
        var_ready, std_ready, shift_ready = sem("var_ready"), sem("std_ready"), sem("shift_ready")
        xn_ready, xn_stored = sem("xn_ready"), sem("xn_stored")
        xnT_ps, xnT_sb, logits_ps = sem("xnT_ps"), sem("xnT_sb"), sem("logits_ps")
        chosen_ready, counts_ps, before_ps = sem("chosen_ready"), sem("counts_ps"), sem("before_ps")
        stats_ready = sem("stats_ready")
        att_var, att_rstd, ln3_root, ln3_step, ln3_ready = map(
            sem, ("att_var", "att_rstd", "ln3_root", "ln3_step", "ln3_ready"))
        hi_ready, pair_ready, bias_split = sem("hi_ready"), sem("pair_ready"), sem("bias_split")
        y0_weighted, x_first, inter_ps = sem("y0_weighted"), sem("x_first"), sem("inter_ps")
        hot_ready, back_ps, table_ready = sem("hot_ready"), sem("back_ps"), sem("table_ready")
        lo_ready, off_ready, act_hot_ready = sem("lo_ready"), sem("off_ready"), sem("act_hot_ready")
        gap_ready, gap_exp_ready = sem("gap_ready"), sem("gap_exp_ready")
        gathered = [sem(f"gathered{r}") for r in range(RING)]
        scattered = [sem(f"scattered{r}") for r in range(RING)]
        xg_ps, xg_sb, h_ps, h_biased, h_gelu = map(sem, ("xg_ps", "xg_sb", "h_ps", "h_biased", "h_gelu"))
        y_ps, y_sb = map(sem, ("y_ps", "y_sb"))
        y_loaded = [[sem(f"y_loaded{k}_{c}") for c in range(NC)] for k in range(TOPK)]
        xa_sb, xa_ps, xaT_sb, qkv_ps = map(sem, ("xa_sb", "xa_ps", "xaT_sb", "qkv_ps"))
        neg_sb, exp_sb, v_sb, phi_sb = map(sem, ("neg_sb", "exp_sb", "v_sb", "phi_sb"))
        qT_ps, qT_sb, kv_sb, prefix_ps = map(sem, ("qT_ps", "qT_sb", "kv_sb", "prefix_ps"))
        state_ps, state_sb = map(sem, ("state_ps", "state_sb"))
        prod_sb, local_sb, nd_sb, den_sb, rden_sb = map(sem, ("prod_sb", "local_sb", "nd_sb", "den_sb", "rden_sb"))
        merged_sb, m_ps, mT_sb, proj_ps, x_attn = map(sem, ("merged_sb", "m_ps", "mT_sb", "proj_ps", "x_attn"))
        x_final, out_stored = sem("x_final"), sem("out_stored")

        xg_bank = banks[:, 0, 0:P]
        def y_bank(r): return banks[:, 5 + r, 0:P]
        def h_bank(r): return banks[:, 2 + r, :]
        w_allT_bank = banks[:, 1, 0:P]
        def xnT_bank(c): return banks[:, 2 + c, :]
        PARTS = (((0, NT // 2), (NT // 2, NT)), ((0, NT - CH), (NT - CH, NT)))

        def logit_bank(f, k):
            bank, first = (((6, 0), (0, 0)), ((3, H * VE), (0, 0)))[f][k]
            return banks[:, bank, first:first + NT * E]

        def parts_done(f, k):
            return len(PARTS[0]) * f + k + 1

        before_bank = banks[:, 7, 0:NT * E]
        count_bank = banks[:, 1, 0:E]
        back_bank = banks[:, 0, 0:2 * NS]
        prefix_bank = banks[:, 0:3, 0:VE // 3 * P]
        qkv_bank = banks[:, 4, 0:QD]
        xa_bank, qT_bank, xn_bank = banks[:, 5, 0:P], banks[:, 5, P:2 * P], banks[:, 4, QD:QD + P]
        def xn_tail_bank(t): return banks[:, (1, 2, 4, 5)[t % 4], 0:P]
        inter_bank = banks[:, 3, 0:H * VE]
        proj_bank, m_bank = banks[:, 6, 0:P], banks[:, 6, P:2 * P]
        state_bank = banks[:, 7, 0:H * VE]

        def slots(eng, body):
            for r in range(RING):
                body(r, r)
            with eng.Fori(1, NS // RING - 1) as j:
                for r in range(RING):
                    body(j * RING + r, r)
            for r in range(RING):
                body(NS - RING + r, r)

        block = ctx.enter_context(nc.Block())

        @block.sync
        def _(sp):
            x_v = x_d[0].rearrange("(t p) d -> p t d", p=P)
            for c in range(NC):
                sp.dma_start(x[:, c * CH:(c + 1) * CH, :], x_v[:, c * CH:(c + 1) * CH, :]).then_inc(x_in[c], 16)
            sp.dma_start(wg[:, :], Wg).then_inc(wg_in, 16)
            sp.dma_start(w2[:, :].rearrange("p (e n) -> p e n", n=P),
                         W2.rearrange("e (c p) d -> p (e c) d", p=P)).then_inc(w2_in, 16)
            for t in range(NT):
                sp.dma_start(b2_rep[t * E:(t + 1) * E, :], b2).then_inc(b2_in, 16)
            for k, w in enumerate((Wq, Wk, Wv, Wo)):
                sp.dma_start(w_raw[:, k, :], w).then_inc(attn_in, 16)
            for k, b in enumerate((bq, bk, bv, bo)):
                for a in range(2):
                    sp.dma_start(bias[a:a + 1, k * P:(k + 1) * P], b.rearrange("(a d) -> a d", a=1)).then_inc(attn_in, 16)
            for f in range(2):
                if f == 0:
                    rows = xn_rows[0].rearrange("(t p) d -> p t d", p=P)
                    for c in range(NC):
                        sp.wait_ge(xn_ready, CH * (c + 1))
                        sp.dma_start(rows[:, c * CH:(c + 1) * CH, :], xn[:, c * CH:(c + 1) * CH, :]).then_inc(xn_stored, 16)
                else:
                    rows = xn_rows[1].rearrange("(t p) d -> t p d", p=P)
                    with sp.Fori(0, NT // 2) as j:
                        for r in range(2):
                            t = 2 * j + r
                            sp.wait_ge(xn_ready, t + (NT + 1))
                            sp.wait_ge(xn_stored, t * 16 + 16 * NC)
                            sp.dma_start(rows[bass.ds(t, 1), :, :].rearrange("a p d -> (a p) d"),
                                         xn_ring[:, r, :]).then_inc(xn_stored, 16)
                sp.wait_ge(experts_ready, f + 1)
                base = NS * f

                def stage(i, r):
                    e = sp.value_load(expert_i[0:1, bass.ds(i, 1)], min_val=0, max_val=E - 1)
                    at_least(sp, h_ps, base + i - RING + 1)
                    at_least(sp, h_biased, base + i - RING + 1)
                    sp.dma_start(w1b[:, r, :], W1b[bass.ds(e, 1), :, :].rearrange("a p n -> (a p) n")).then_inc(w1b_in[r], 16)

                slots(sp, stage)
                for r in range(RING):
                    sp.wait_ge(scattered[r], 16 * (NS // RING) * (f + 1))
                back_rows = y_rows[f].rearrange("(k t p) d -> k p t d", k=TOPK, p=P)
                for k, c in ((0, 0), *((k, c + 1 - k) for c in range(NC - 1) for k in range(TOPK)), (1, NC - 1)):
                    sp.dma_start(y_back[:, k, c * CH:(c + 1) * CH, :],
                                 back_rows[k, :, c * CH:(c + 1) * CH, :]).then_inc(y_loaded[k][c], 16)
            out_v = out_d[0].rearrange("(t p) d -> p t d", p=P)
            for c in range(NC):
                sp.wait_ge(x_final, CH * (c + 1))
                sp.dma_start(out_v[:, c * CH:(c + 1) * CH, :], x[:, c * CH:(c + 1) * CH, :]).then_inc(out_stored, 16)
            sp.wait_ge(out_stored, 16 * NC)

        @block.gpsimd
        def _(pool):
            g = nc.gpsimd
            g.memset(ident[:, :], 0.0).then_inc(const_step, 1)
            g.memset(tri[:, :], 1.0).then_inc(const_step, 1)
            g.memset(strict_bf[:, :], 1.0).then_inc(const_step, 1)
            g.memset(before[:, :, :], 1.0).then_inc(const_step, 1)
            g.memset(head_mask[:, :, :], 1.0).then_inc(const_step, 1)
            pool.wait_ge(const_step, 5)
            g.affine_select(out=ident[:, :], in_=ident[:, :], compare_op=ALU.not_equal, fill=1.0, base=0,
                            pattern=[[-1, P]], channel_multiplier=1).then_inc(consts, 1)
            g.memset(ones_bf[:, :], 1.0).then_inc(consts, 1)
            g.memset(ones2[:, :].bitcast(F32), 1.0).then_inc(consts, 1)
            g.affine_select(out=before[:, :, :], in_=before[:, :, :], compare_op=ALU.is_ge, fill=0.0, base=-1,
                            pattern=[[1, E], [-1, E]], channel_multiplier=0).then_inc(consts, 1)
            g.affine_select(out=strict_bf[:, :], in_=strict_bf[:, :], compare_op=ALU.is_ge, fill=0.0, base=-1,
                            pattern=[[1, P]], channel_multiplier=-1).then_inc(consts, 1)
            flt = dict(allow_small_or_imprecise_dtypes=True)
            g.iota(slot_no[:, :], pattern=[[1, NS]], base=0, channel_multiplier=0, **flt).then_inc(consts, 1)
            g.iota(lane_no[:, :], pattern=[[1, P]], base=0, channel_multiplier=0, **flt).then_inc(consts, 1)
            g.iota(full_tiles[:, :], pattern=[[P, NT]], base=0, channel_multiplier=0, **flt).then_inc(consts, 1)
            g.iota(pair_no[:, :], pattern=[[1, TOPK * NT]], base=1, channel_multiplier=0, **flt).then_inc(consts, 1)
            g.iota(own_lane[:, :], pattern=[[0, 1]], base=0, channel_multiplier=1, **flt).then_inc(consts, 1)
            g.affine_select(out=tri[:, :], in_=tri[:, :], compare_op=ALU.is_ge, fill=0.0, base=0,
                            pattern=[[1, P]], channel_multiplier=-1).then_inc(consts, 1)
            g.affine_select(out=head_mask[:, :, :], in_=head_mask[:, :, :], compare_op=ALU.is_ge, fill=0.0, base=0,
                            pattern=[[0, VE], [-DH, H]], channel_multiplier=1).then_inc(const_step, 1)
            pool.wait_ge(const_step, 6)
            g.affine_select(out=head_mask[:, :, :], in_=head_mask[:, :, :], compare_op=ALU.is_ge, fill=0.0,
                            base=DH - 1, pattern=[[0, VE], [DH, H]], channel_multiplier=-1).then_inc(consts, 1)
            g.memset(tile_mask[:, :], 1.0).then_inc(const_step, 1)
            pool.wait_ge(const_step, 7)
            g.affine_select(out=tile_mask[:, :], in_=tile_mask[:, :], compare_op=ALU.is_ge, fill=0.0, base=0,
                            pattern=[[-E, NT]], channel_multiplier=1).then_inc(const_step, 1)
            pool.wait_ge(const_step, 8)
            g.affine_select(out=tile_mask[:, :], in_=tile_mask[:, :], compare_op=ALU.is_ge, fill=0.0, base=E - 1,
                            pattern=[[E, NT]], channel_multiplier=-1).then_inc(const_step, 1)
            g.memset(minus_half[:, :], -0.5).then_inc(const_step, 1)
            g.memset(halves_scale[:, :, 0], -0.5).then_inc(const_step, 1)
            g.memset(halves_scale[:, :, 1], 1.0 / D).then_inc(const_step, 1)
            g.memset(quarter[:, :], 0.25).then_inc(const_step, 1)
            g.memset(eps[:, :], LN_EPS).then_inc(const_step, 1)
            pool.wait_ge(const_step, 14)
            g.memset(vx[:, :, :, :], 1.0).then_inc(consts, 1)
            g.memset(state[:, :], 0.0).then_inc(consts, 1)
            pool.wait_ge(b2_in, 16 * NT)
            g.tensor_tensor(b2_blk[:, :, :], b2_rep[:, :].unsqueeze(1).to_broadcast([P, NT, P]),
                            tile_mask[:, :].unsqueeze(2).to_broadcast([P, NT, P]), ALU.mult).then_inc(b2_blk_ready, 1)

            def ffn_moves(f):
                for a in range(0, KT, KT // 4):
                    pool.wait_ge(hi_ready, 2 * f + 2 * a // KT + 1)
                    b = a + KT // 4
                    g.tensor_tensor(hi_val[:, a:b, 1, :], hi_hot[:, a:b, :],
                                    pair_no[:, a:b].unsqueeze(2).to_broadcast([P, KT // 4, NS]), ALU.mult).then_inc(pair_ready, 1)
                for q in range(POOL_Q, KT):
                    g.tensor_scalar(lo_hot[:, q, :], lane_no[:, :], lo_f[:, q:q + 1], None,
                                    ALU.is_equal).then_inc(pair_ready, 1)
                pool.wait_ge(xn_stored, 16 * (NC + NT * f))
                pool.wait_ge(table_ready, f + 1)
                lag = 7
                for n in range(NS + lag):
                    if n < NS:
                        at_least(pool, xg_ps, NS * f + n - RING + 1)
                        g.indirect_dma_start(
                            out=xg[:, n % RING, :], out_offset=None, in_=xn_rows[f][:, :],
                            in_offset=bass.IndirectOffsetOnAxis(ap=src_row[:, n:n + 1], axis=0),
                        ).then_inc(gathered[n % RING], 16)
                    i = n - lag
                    if i >= 0:
                        pool.wait_ge(y_sb, NS * f + i + 1)
                        g.indirect_dma_start(
                            out=y_rows[f][:, :],
                            out_offset=bass.IndirectOffsetOnAxis(ap=dst_row[:, i:i + 1], axis=0),
                            in_=y_tile[:, i % RING, :], in_offset=None,
                            bounds_check=TOPK * T - 1, oob_is_err=False,
                        ).then_inc(scattered[i % RING], 16)

            def reciprocal_root(k, a, b):
                pool.wait_ge(att_var, k + 1)
                g.tensor_tensor(rstd[:, a:b], var[:, a:b], minus_half[:, a:b], ALU.pow).then_inc(att_rstd, 1)

            def add_first(f):
                for t in range(0, NT, 2):
                    if t % CH == 0:
                        pool.wait_ge(b2_added, NC * f + t // CH + 1)
                    pool.wait_ge(y0_weighted, NT * f + t + 2)
                    g.tensor_tensor(y_back[:, 0, t:t + 2, :], y_back[:, 0, t:t + 2, :], x[:, t:t + 2, :],
                                    ALU.add).then_inc(x_first, 1)
                    if f == 0 and t == CH + 2:
                        reciprocal_root(0, 0, CH)

            ffn_moves(0)
            add_first(0)

            def outer(i, r):
                pool.wait_ge(phi_sb, i + 1)
                pool.wait_ge(v_sb, i + 1)
                at_least(pool, prefix_ps, i - 1)
                k4 = qk[:, r, P:2 * P].rearrange("p (h d) -> p h d", h=H).unsqueeze(1).to_broadcast([P, DH, H, DH])
                v4 = vx[:, r, 0:DH, :].unsqueeze(3).to_broadcast([P, DH, H, DH])
                o4 = kv[:, r, :, :].rearrange("p e (h d) -> p e h d", h=H)
                g.tensor_tensor(o4, k4, v4, ALU.mult).then_inc(kv_sb, 1)

            def ln3_moments(j, t=None, n=2):
                t = j * 2 if t is None else t
                pool.wait_ge(stats_ready, t + (NT + n))
                at_least(pool, ln3_ready, j if isinstance(j, int) else 0)
                st, cols = stats[:, bass.ds(t, n), :], bass.ds(t, n)
                halves, apart, quarter_apart, var_n = halves_3[:, 0:n, :], apart_3[:, 0:n], apart_quarter_3[:, 0:n], var_3[:, 0:n]
                g.tensor_tensor(halves, st[:, :, 1:3], st[:, :, 4:6], ALU.add).then_inc(ln3_step, 1)
                g.tensor_tensor(apart, st[:, :, 1], st[:, :, 4], ALU.subtract).then_inc(ln3_step, 1)
                pool.wait_ge(ln3_step, j * 7 + 2)
                g.tensor_tensor(halves, halves, halves_scale[:, 0:n, :], ALU.mult).then_inc(ln3_step, 1)
                g.tensor_tensor(quarter_apart, apart, quarter[:, 0:n], ALU.mult).then_inc(ln3_step, 1)
                pool.wait_ge(ln3_step, j * 7 + 4)
                g.tensor_tensor(apart, apart, quarter_apart, ALU.mult).then_inc(ln3_step, 1)
                g.tensor_tensor(var_n, halves[:, :, 1], eps[:, 0:n], ALU.add).then_inc(ln3_step, 1)
                pool.wait_ge(ln3_step, j * 7 + 6)
                g.tensor_tensor(var_n, var_n, apart, ALU.add).then_inc(ln3_step, 1)
                pool.wait_ge(ln3_step, j * 7 + 7)
                g.tensor_tensor(rstd_3[:, cols], var_n, minus_half[:, 0:n], ALU.pow).then_inc(ln3_root, 1)
                pool.wait_ge(ln3_root, j + 1)
                g.tensor_tensor(shift_3[:, cols], halves[:, :, 0], rstd_3[:, cols], ALU.mult).then_inc(ln3_ready, 1)

            outer(0, 0)
            reciprocal_root(1, CH, NT)
            outer(1, 1)
            outer(2, 0)
            outer(3, 1)
            with pool.Fori(2, NT // 2) as j:
                outer(2 * j, 0)
                ln3_moments(j - 2)
                outer(2 * j + 1, 1)
            ln3_moments(NT // 2 - 2)
            ln3_moments(NT // 2 - 1, NT - 2, 1)
            ln3_moments(NT // 2, NT - 1, 1)
            ffn_moves(1)
            add_first(1)

        @block.scalar
        def _(act):
            s = nc.scalar

            def ffn(f):
                if f == 0:
                    for half in range(2):
                        act.wait_ge(var_ready, half + 1)
                        cols = slice(half * NT // 2, (half + 1) * NT // 2)
                        s.activation(std[:, cols], var[:, cols], ACT.Sqrt).then_inc(std_ready, 1)
                        for c in range(half * NC // 2, (half + 1) * NC // 2):
                            act.wait_ge(xnT_ps, c + 1)
                            s.copy(xnT[:, c * CH * P:(c + 1) * CH * P], xnT_bank(c)).then_inc(xnT_sb, 1)
                if f == 0:
                    act.wait_ge(attn_w_ps, 1)
                    s.copy(w_attn[:, :, :].rearrange("p k n -> p (k n)"), banks[:, 7, :]).then_inc(attn_w_sb, 1)
                act.wait_ge(lo_ready, f + 1)
                for q in range(ACT_Q, POOL_Q):
                    ins = s.activation(off[:, q - ACT_Q, :], lane_no[:, :], ACT.Square, scale=-1.0,
                                       bias=lo_f[:, q:q + 1])
                ins.then_inc(off_ready, 1)
                act.wait_ge(off_ready, f + 1)
                s.activation(lo_hot[:, ACT_Q:POOL_Q, :], off[:, :, :], ACT.Relu, scale=-1.0,
                             bias=tri[:, P - 1:P]).then_inc(act_hot_ready, 1)
                s.activation(warm[:, f, 0:1], tri[:, 0:1], ACT.Exp)
                act.wait_ge(gap_ready, f + 1)
                s.activation(gap_exp[:, :], gap[:, :], ACT.Exp).then_inc(gap_exp_ready, 1)
                s.activation(warm[:, f, 1:2], tri[:, 0:1], ACT.Gelu_apprx_tanh)
                base = NS * f

                def rows(i, r):
                    act.wait_ge(xg_ps, base + i + 1)
                    at_least(act, h_ps, base + i - RING + 1)
                    s.copy(xgT[:, r, :], xg_bank).then_inc(xg_sb, 1)

                def step(i, r, lead=True):
                    if lead:
                        rows(i + 2, (r + 2) % RING)
                    act.wait_ge(h_biased, base + i + 1)
                    at_least(act, y_ps, base + i - RING + 1)
                    s.activation(h_act[:, r, :], h_pre[:, r, :], ACT.Gelu_apprx_tanh).then_inc(h_gelu, 1)

                rows(0, 0)
                rows(1, 1)
                for r in range(RING):
                    step(r, r)
                with act.Fori(1, NS // RING - 1) as j:
                    for r in range(RING):
                        step(j * RING + r, r)
                for r in range(RING):
                    step(NS - RING + r, r, lead=(r + 2 < RING))
                if f == 0:
                    s.activation(warm[:, f, 2:3], tri[:, 0:1], ACT.Exp)
                act.wait_ge(w_allT_ps, f + 1)
                s.copy(w_allT[:, :], w_allT_bank).then_inc(w_allT_sb, 1)
                for t in range(NT):
                    if t % CH == 0:
                        act.wait_ge(y_loaded[0][t // CH], 16 * (f + 1))
                    s.activation(y_back[:, 0, t, :], y_back[:, 0, t, :], ACT.Copy,
                                 scale=half_w[:, 0, t:t + 1]).then_inc(y0_weighted, 1)

            ffn(0)

            def norm_3(j, r):
                t = 2 * j + r
                act.wait_ge(ln3_ready, j + (2 if isinstance(t, int) and t == NT - 1 else 1))
                if not (isinstance(j, int) and j == 0):
                    act.wait_ge(xnT_ps, t + (NC - 1))
                    act.wait_ge(xn_stored, t * 16 + 16 * (NC - 1))
                s.activation(xn_ring[:, r, :], x[:, bass.ds(t, 1), :].rearrange("p a d -> p (a d)"), ACT.Identity,
                             bias=shift_3[:, bass.ds(t, 1)], scale=rstd_3[:, bass.ds(t, 1)]).then_inc(xn_ready, 1)

            def turned_3(j, r, bank):
                act.wait_ge(xnT_ps, 2 * j + r + (NC + 1))
                s.copy(xnT[:, r * P:(r + 1) * P], bank).then_inc(xnT_sb, 1)

            def norm(i, r):
                if isinstance(i, int) and i == CH:
                    act.wait_ge(shift_ready, 2)
                at_least(act, xa_ps, i - 1)
                s.activation(xa[:, r, :], x[:, bass.ds(i, 1), :].rearrange("p a d -> p (a d)"), ACT.Identity,
                             bias=shift[:, bass.ds(i, 1)], scale=rstd[:, bass.ds(i, 1)]).then_inc(xa_sb, 1)

            def pre(i, r, gate=None):
                act.wait_ge(xa_ps, i + 1)
                at_least(act, qkv_ps, i - 1)
                s.copy(xaT[:, r, :], xa_bank).then_inc(xaT_sb, 1)
                act.wait_ge(qkv_ps, i + 1)
                at_least(act, exp_sb, i - 1)
                s.activation(neg[:, r, :], qkv_bank[:, 0:2 * P], ACT.Relu, scale=-1.0).then_inc(neg_sb, 1)
                at_least(act, kv_sb, i - 1)
                at_least(act, state_ps, i - 1)
                s.copy(vx[:, r, 0:DH, :], qkv_bank[:, 2 * P:QD].rearrange("p (h d) -> p d h", h=H)).then_inc(v_sb, 1)
                if gate is not None:
                    turned_3(gate, r, xn_bank)
                act.wait_ge(neg_sb, i + 1)
                at_least(act, phi_sb, i - 1)
                s.activation(expo[:, r, :], neg[:, r, :], ACT.Exp, scale=-1.0).then_inc(exp_sb, 1)

            def post(i, r):
                act.wait_ge(m_ps, i + 1)
                at_least(act, proj_ps, i - 1)
                s.copy(mT[:, r, :], m_bank).then_inc(mT_sb, 1)

            act.wait_ge(consts, 14)
            act.wait_ge(shift_ready, 1)
            norm(0, 0)
            norm(1, 1)
            pre(0, 0)
            pre(1, 1)
            norm(2, 0)

            def attn(j, r, lead=True):
                i = 2 * j + r
                known = isinstance(j, int)
                act.wait_ge(qT_ps, i + 1)
                at_least(act, inter_ps, i - 1)
                s.copy(qT[:, r, :], qT_bank).then_inc(qT_sb, 1)
                gate = None if known and j < 2 else j - 2
                if gate is not None:
                    norm_3(gate, r)
                if not (known and i == 0):
                    post(i - 1, 1 - r)
                if lead:
                    pre(i + 2, r, gate)
                else:
                    turned_3(gate, r, xn_bank)
                if not (known and i + 3 >= NT):
                    norm(i + 3, 1 - r)

            for j in range(2):
                for r in range(2):
                    attn(j, r)
            with act.Fori(2, NT // 2 - 2) as j:
                for r in range(2):
                    attn(j, r)
            for i in range(NT - 4, NT):
                attn(i // 2, i % 2, lead=(i < NT - 2))
            for r in range(2):
                norm_3(NT // 2 - 2, r)
            for r in range(2):
                turned_3(NT // 2 - 2, r, xn_tail_bank(r))
            post(NT - 1, (NT - 1) % 2)
            norm_3(NT // 2 - 1, 0)
            turned_3(NT // 2 - 1, 0, xn_tail_bank(2))
            norm_3(NT // 2 - 1, 1)
            turned_3(NT // 2 - 1, 1, xn_tail_bank(3))
            ffn(1)

        @block.vector
        def _(dve):
            v = nc.vector
            steps = [0]

            def link(ins):
                steps[0] += 1
                ins.then_inc(dve_step, 1)
                dve.wait_ge(dve_step, steps[0])

            def variance(a, b, done):
                me, mo = stats[:, a:b, 1], stats[:, a:b, 4]
                v.tensor_tensor(m_sum[:, a:b], me, mo, ALU.add).then_inc(dve_step, 1)
                v.tensor_tensor(v_sum[:, a:b], stats[:, a:b, 2], stats[:, a:b, 5], ALU.add).then_inc(dve_step, 1)
                steps[0] += 2
                link(v.tensor_tensor(m_dif[:, a:b], me, mo, ALU.subtract))
                v.tensor_scalar(mean[:, a:b], m_sum[:, a:b], 0.5, None, ALU.mult).then_inc(dve_step, 1)
                steps[0] += 1
                link(v.scalar_tensor_tensor(out=v_dif[:, a:b], in0=m_dif[:, a:b], scalar=0.25, in1=m_dif[:, a:b],
                                            op0=ALU.mult, op1=ALU.mult))
                link(v.scalar_tensor_tensor(out=v_dif[:, a:b], in0=v_sum[:, a:b], scalar=1.0 / D, in1=v_dif[:, a:b],
                                            op0=ALU.mult, op1=ALU.add))
                v.tensor_scalar(var[:, a:b], v_dif[:, a:b], LN_EPS, None, ALU.add).then_inc(done, 1)

            def attention_shift(k, a, b):
                dve.wait_ge(att_rstd, k + 1)
                v.scalar_tensor_tensor(out=shift[:, a:b], in0=mean[:, a:b], scalar=-1.0, in1=rstd[:, a:b],
                                       op0=ALU.mult, op1=ALU.mult).then_inc(shift_ready, 1)

            def gate_and_route(f):
                if f == 0:
                    dve.wait_ge(consts, 14)
                for k, (a, b) in enumerate(PARTS[f]):
                    n = b - a
                    dve.wait_ge(logits_ps, parts_done(f, k))
                    link(v.tensor_copy(logit[:, a:b, :].rearrange("p t e -> p (t e)"),
                                       logit_bank(f, k)[:, a * E:b * E]))
                    for e in range(E):
                        if e:
                            v.tensor_tensor(beats[:, a:b, e, 0:e], logit[:, a:b, 0:e],
                                            logit[:, a:b, e:e + 1].to_broadcast([P, n, e]), ALU.is_ge).then_inc(dve_step, 1)
                        v.tensor_tensor(beats[:, a:b, e, e:E], logit[:, a:b, e:E],
                                        logit[:, a:b, e:e + 1].to_broadcast([P, n, E - e]), ALU.is_gt).then_inc(dve_step, 1)
                    steps[0] += 2 * E - 1
                    dve.wait_ge(dve_step, steps[0])
                    link(v.tensor_reduce(rank[:, a:b, :], beats[:, a:b, :, :], AX.X, ALU.add))
                    v.tensor_scalar(chosen[:, a:b, :], rank[:, a:b, :], float(TOPK), None, ALU.is_lt).then_inc(chosen_ready, 1)
                v.tensor_scalar(is_rank[:, 0, :, :], rank[:, :, :], 0.0, None, ALU.is_equal).then_inc(dve_step, 1)
                steps[0] += 1
                link(v.tensor_scalar(is_rank[:, 1, :, :], rank[:, :, :], 1.0, None, ALU.is_equal))
                dve.wait_ge(counts_ps, f + 1)
                link(v.tensor_tensor(more[:, :, :], count_bank.unsqueeze(2).to_broadcast([P, E, NT]),
                                     full_tiles[:, :].unsqueeze(1).to_broadcast([P, E, NT]), ALU.is_gt))
                link(v.tensor_reduce(tiles_of[:, :], more[:, :, :], AX.X, ALU.add))
                link(v.tensor_tensor(below[:, :, :], before[:, :, :],
                                     tiles_of[:, :].unsqueeze(1).to_broadcast([P, E, E]), ALU.mult))
                link(v.tensor_reduce(first_tile[:, :], below[:, :, :], AX.X, ALU.add))
                v.tensor_tensor(end_tile[:, :], first_tile[:, :], tiles_of[:, :], ALU.add).then_inc(dve_step, 1)
                steps[0] += 1
                link(v.tensor_scalar(first_tile[:, :], first_tile[:, :], float(P), None, ALU.mult))
                dve.wait_ge(before_ps, f + 1)
                link(v.tensor_tensor(slot[:, :, :], before_bank.rearrange("p (t e) -> p t e", e=E),
                                     first_tile[:, :].unsqueeze(1).to_broadcast([P, NT, E]), ALU.add))
                link(v.tensor_tensor(picked[:, :, :, :], is_rank[:, :, :, :],
                                     slot[:, :, :].unsqueeze(1).to_broadcast([P, TOPK, NT, E]), ALU.mult))
                with nc.allow_low_precision(reason="whole numbers below 2 ** 24, summed in float32"):
                    link(v.tensor_reduce(pos_i[:, :], picked[:, :, :, :].rearrange("p k t e -> p (k t) e"),
                                         AX.X, ALU.add))
                v.tensor_scalar(hi_i[:, :], pos_i[:, :], 7, None, ALU.logical_shift_right).then_inc(dve_step, 1)
                steps[0] += 1
                link(v.tensor_scalar(lo_i[:, :], pos_i[:, :], P - 1, None, ALU.bitwise_and))
                v.tensor_copy(hi_f[:, :], hi_i[:, :]).then_inc(dve_step, 1)
                steps[0] += 1
                v.tensor_copy(lo_f[:, :], lo_i[:, :]).then_inc(lo_ready, 1)
                dve.wait_ge(dve_step, steps[0])
                dve.wait_ge(lo_ready, f + 1)
                for a in (0, KT // 2):
                    v.tensor_tensor(hi_hot[:, a:a + KT // 2, :], slot_no[:, :].unsqueeze(1).to_broadcast([P, KT // 2, NS]),
                                    hi_f[:, a:a + KT // 2].unsqueeze(2).to_broadcast([P, KT // 2, NS]),
                                    ALU.is_equal).then_inc(hi_ready, 1)
                dve.wait_ge(hi_ready, 2 * f + 2)
                v.tensor_scalar(hi_val[:, :, 0, :], hi_hot[:, :, :], own_lane[:, 0:1], None,
                                ALU.mult).then_inc(hot_ready, 1)
                for a, b in HOTS:
                    v.tensor_tensor(lo_hot[:, a:b, :], lane_no[:, :].unsqueeze(1).to_broadcast([P, b - a, P]),
                                    lo_f[:, a:b].unsqueeze(2).to_broadcast([P, b - a, P]),
                                    ALU.is_equal).then_inc(hot_ready, 1)
                link(v.tensor_tensor(past[:, :, :], slot_no[:, :].unsqueeze(2).to_broadcast([P, NS, E]),
                                     end_tile[:, :].unsqueeze(1).to_broadcast([P, NS, E]), ALU.is_ge))
                link(v.tensor_reduce(expert_f[:, :], past[:, :, :], AX.X, ALU.add))
                v.tensor_scalar(expert_i[:, :], expert_f[:, :], float(E - 1), None, ALU.min).then_inc(experts_ready, 1)
                dve.wait_ge(back_ps, f + 1)
                link(v.tensor_copy(back[:, :], back_bank))
                v.tensor_scalar(empty[:, :], back[:, NS:2 * NS], 0.0, float(PAD), ALU.is_equal, ALU.mult).then_inc(dve_step, 1)
                steps[0] += 1
                link(v.scalar_tensor_tensor(out=row_f[:, :], in0=back[:, NS:2 * NS], scalar=float(P), in1=back[:, 0:NS],
                                            op0=ALU.mult, op1=ALU.add))
                link(v.scalar_tensor_tensor(out=dst_row[:, :], in0=row_f[:, :], scalar=-float(P), in1=empty[:, :],
                                            op0=ALU.add, op1=ALU.add))
                v.tensor_scalar(src_row[:, :], dst_row[:, :], T - 1, None, ALU.bitwise_and).then_inc(table_ready, 1)
                v.tensor_scalar(expert_w[:, :], expert_f[:, :], float(E - 1), float(DF), ALU.min, ALU.mult).then_inc(expert_w_ready, 1)
                both = logit[:, :, :].unsqueeze(1).to_broadcast([P, TOPK, NT, E])
                link(v.tensor_tensor(picked[:, :, :, :], is_rank[:, :, :, :], both, ALU.mult))
                link(v.tensor_reduce(top[:, :, :], picked[:, :, :, :], AX.X, ALU.add))
                v.tensor_tensor(gap[:, :], top[:, 1, :], top[:, 0, :], ALU.subtract).then_inc(gap_ready, 1)
                dve.wait_ge(gap_exp_ready, f + 1)
                link(v.tensor_scalar(gap_den[:, :], gap_exp[:, :], 1.0, 2.0, ALU.add, ALU.mult))
                link(v.reciprocal(half_w[:, 0, :], gap_den[:, :]))
                link(v.tensor_tensor(half_w[:, 1, :], half_w[:, 0, :], gap_exp[:, :], ALU.mult))
                link(v.tensor_tensor(w_pair[:, :, :, :], is_rank[:, :, :, :],
                                     half_w[:, :, :].unsqueeze(3).to_broadcast([P, TOPK, NT, E]), ALU.mult))
                v.tensor_tensor(w_all[:, :, :], w_pair[:, 0, :, :], w_pair[:, 1, :, :], ALU.add).then_inc(w_all_ready, 1)

            def experts(f):
                base = NS * f

                def hidden(i, r):
                    dve.wait_ge(h_ps, base + i + 1)
                    at_least(dve, h_gelu, base + i - RING + 1)
                    v.tensor_tensor(h_pre[:, r, :].rearrange("p (c n) -> p c n", c=FC),
                                    h_bank(r).rearrange("p (c n) -> p c n", c=FC),
                                    w1b[:, r, DF:DF + FC].unsqueeze(2).to_broadcast([P, FC, P]),
                                    ALU.add).then_inc(h_biased, 1)

                def output(j, r):
                    i = j * RING + r
                    dve.wait_ge(y_ps, base + i + 1)
                    at_least(dve, scattered[r], j * 16 + 16 * (NS // RING) * f)
                    v.tensor_copy(y_tile[:, r, :], y_bank(r)).then_inc(y_sb, 1)

                LAG = 2
                hidden(0, 0)
                hidden(1, 1)
                hidden(2, 2)
                output(0, 0)
                if f == 0:
                    dve.wait_ge(attn_in, 16 * 12)
                    v.tensor_scalar(row_0[:, :], own_lane[0:2, :], 0.0, None, ALU.is_equal).then_inc(dve_step, 1)
                    steps[0] += 1
                    link(v.tensor_copy(bias_hi[:, :], bias[:, :]))
                    link(v.tensor_tensor(bias_lo[:, :], bias[:, :], bias_hi[:, :].bitcast(F32), ALU.subtract))
                    link(v.tensor_scalar(bias_lo[:, :], bias_lo[:, :], own_lane[0:2, 0:1], None, ALU.mult))
                    v.scalar_tensor_tensor(out=bias_2[:, :], in0=bias_hi[:, :].bitcast(F32), scalar=row_0[:, 0:1],
                                           in1=bias_lo[:, :], op0=ALU.mult, op1=ALU.add).then_inc(bias_split, 1)
                with dve.Fori(1, NS // RING) as j:
                    for r in range(RING):
                        hidden(j * RING + r, r)
                        output(j if r >= LAG else j - 1, (r - LAG) % RING)
                output(NS // RING - 1, RING - 2)
                output(NS // RING - 1, RING - 1)

            def phi(i, r):
                dve.wait_ge(exp_sb, i + 1)
                at_least(dve, local_sb, i - 1)
                at_least(dve, kv_sb, i - 1)
                at_least(dve, state_ps, i - 1)
                v.scalar_tensor_tensor(out=qk[:, r, :], in0=qkv_bank[:, 0:2 * P], scalar=0.0, in1=expo[:, r, :],
                                       op0=ALU.max, op1=ALU.add).then_inc(phi_sb, 1)

            def combine(f):
                for c in range(NC):
                    dve.wait_ge(b2_ps, NC * f + c + 1)
                    xc = x[:, c * CH:(c + 1) * CH, :].rearrange("p t d -> p (t d)")
                    v.tensor_tensor(xc, banks[:, 2 + c, :], xc, ALU.add).then_inc(b2_added, 1)
                for t in range(NT):
                    dve.wait_ge(x_first, (NT * f + t) // 2 + 1)
                    if t % CH == 0:
                        dve.wait_ge(y_loaded[1][t // CH], 16 * (f + 1))
                    v.scalar_tensor_tensor(out=x[:, t, :], in0=y_back[:, 1, t, :],
                                           scalar=half_w[:, 1, t:t + 1], in1=y_back[:, 0, t, :],
                                           op0=ALU.mult, op1=ALU.add).then_inc(x_final if f else x_mid, 1)
                    if f == 0 and t:
                        dve.wait_ge(x_mid, t)
                        v.bn_stats(stats[:, t - 1, :], x[:, t - 1, :]).then_inc(stats_ready, 1)
                        if t == CH:
                            dve.wait_ge(stats_ready, CH)
                            variance(0, CH, att_var)
                    if f == 0 and t == NT - 3:
                        phi(0, 0)
                    if f == 0 and t == 2 * CH - 2:
                        attention_shift(0, 0, CH)
                if f == 0:
                    dve.wait_ge(x_mid, NT)
                    v.bn_stats(stats[:, NT - 1, :], x[:, NT - 1, :]).then_inc(stats_ready, 1)
                    dve.wait_ge(stats_ready, NT)
                    variance(CH, NT, att_var)

            v.memset(blank[:, :], 0.0).then_inc(blank_ready, 1)

            def start_half(half):
                a, b = half * NT // 2, (half + 1) * NT // 2
                for t in range(a, b):
                    if t % CH == 0:
                        dve.wait_ge(x_in[t // CH], 16)
                    v.bn_stats(stats[:, t, :], x[:, t, :]).then_inc(dve_step, 1)
                steps[0] += b - a
                dve.wait_ge(dve_step, steps[0])
                variance(a, b, var_ready)
                dve.wait_ge(std_ready, half + 1)
                link(v.reciprocal(rstd[:, a:b], std[:, a:b]))
                for t in range(a, b):
                    v.tensor_scalar(xn[:, t, :], x[:, t, :], mean[:, t:t + 1], rstd[:, t:t + 1],
                                    ALU.subtract, ALU.mult).then_inc(xn_ready, 1)

            start_half(0)
            start_half(1)
            gate_and_route(0)
            experts(0)
            combine(0)

            def attend(i, r):
                first = isinstance(i, int) and i == 0
                dve.wait_ge(prefix_ps, i + 1)
                at_least(dve, local_sb, i)
                q4 = qk[:, r, 0:P].unsqueeze(1).unsqueeze(1).to_broadcast([P, 3, VE // 3, P])
                v.tensor_tensor(prod[:, :].rearrange("p (b e n) -> p b e n", b=3, n=P),
                                prefix_bank.rearrange("p b (e n) -> p b e n", n=P), q4, ALU.mult).then_inc(prod_sb, 1)
                dve.wait_ge(prod_sb, i + 1)
                at_least(dve, nd_sb, i)
                v.tensor_reduce(local[:, :, :].rearrange("p e h -> p (e h)"),
                                prod[:, :].rearrange("p (g d) -> p g d", d=DH), AX.X, ALU.add).then_inc(local_sb, 1)
                dve.wait_ge(local_sb, i + 1)
                dve.wait_ge(inter_ps, i + 1)
                v.tensor_tensor(nd[:, :, :].rearrange("p e h -> p (e h)"), inter_bank,
                                local[:, :, :].rearrange("p e h -> p (e h)"), ALU.add).then_inc(nd_sb, 1)
                if not first:
                    residual(i - 1)
                dve.wait_ge(nd_sb, i + 1)
                v.tensor_scalar(den[:, :], nd[:, DH, :], ATT_EPS, None, ALU.add).then_inc(den_sb, 1)
                dve.wait_ge(state_ps, i + 1)
                v.tensor_tensor(state[:, :], state_bank, head_mask[:, :, :].rearrange("p e h -> p (e h)"),
                                ALU.mult).then_inc(state_sb, 1)
                dve.wait_ge(den_sb, i + 1)
                v.reciprocal(rden[:, :], den[:, :]).then_inc(rden_sb, 1)
                if not first:
                    moments(i - 1)
                dve.wait_ge(rden_sb, i + 1)
                at_least(dve, m_ps, i - 1)
                v.tensor_tensor(merged[:, r, :].rearrange("p (h d) -> p d h", h=H), nd[:, 0:DH, :],
                                rden[:, :].unsqueeze(1).to_broadcast([P, DH, H]), ALU.mult).then_inc(merged_sb, 1)

            def residual(i):
                dve.wait_ge(proj_ps, i + 1)
                xt = x[:, bass.ds(i, 1), :].rearrange("p a d -> p (a d)")
                v.tensor_tensor(xt, proj_bank, xt, ALU.add).then_inc(x_attn, 1)

            def moments(i):
                dve.wait_ge(x_attn, i + 1)
                v.bn_stats(stats[:, bass.ds(i, 1), :].rearrange("p a d -> p (a d)"),
                           x[:, bass.ds(i, 1), :].rearrange("p a d -> p (a d)")).then_inc(stats_ready, 1)

            def attn(i, r, phis=True):
                if phis:
                    phi(i + 1, 1 - r)
                attend(i, r)
                if isinstance(i, int) and i == 0:
                    attention_shift(1, CH, NT)

            for i in range(2):
                attn(i, i)
            with dve.Fori(1, NT // 2 - 1) as j:
                for r in range(2):
                    attn(2 * j + r, r)
            attn(NT - 2, 0)
            attn(NT - 1, 1, phis=False)
            residual(NT - 1)
            moments(NT - 1)

            gate_and_route(1)
            experts(1)
            combine(1)

        @block.tensor
        def _(pe):
            mm = nc.tensor.matmul

            def keep_warm(n, bank=6):
                for _ in range(n):
                    mm(banks[:, bank, :], blank[:, 0:P], blank[:, :], start=True, stop=True)

            pe.wait_ge(blank_ready, 1)
            pe.wait_ge(consts, 14)

            def gate():
                def turn(c):
                    for t in range(c * CH, (c + 1) * CH):
                        pe.wait_ge(xn_ready, t + 1)
                        last = pe.transpose(xnT_bank(c)[:, (t % CH) * P:(t % CH + 1) * P], xn[:, t, :], ident[:, :])
                    last.then_inc(xnT_ps, 1)

                def logits(c):
                    pe.wait_ge(xnT_sb, c + 1)
                    k, = (k for k, (a, b) in enumerate(PARTS[0]) if a <= c * CH < b)
                    bank = logit_bank(0, k)
                    for t in range(c * CH, (c + 1) * CH):
                        last = mm(bank[:, t * E:(t + 1) * E], xnT[:, t * P:(t + 1) * P], wg[:, :], start=True, stop=True)
                    if (c + 1) * CH == PARTS[0][k][1]:
                        last.then_inc(logits_ps, 1)

                pe.wait_ge(wg_in, 16)
                for c in range(0, NC, 2):
                    turn(c)
                    turn(c + 1)
                    logits(c)
                    logits(c + 1)
                pe.wait_ge(attn_in, 16 * 12)
                for k in range(4):
                    last = pe.transpose(banks[:, 7, k * P:(k + 1) * P], w_raw[:, k, :], ident[:, :])
                last.then_inc(attn_w_ps, 1)
                pe.wait_ge(attn_w_sb, 1)

            def route(f):
                for k, (a, b) in enumerate(PARTS[f]):
                    pe.wait_ge(chosen_ready, parts_done(f, k))
                    for t in range(a, b):
                        last = mm(count_bank, ones_bf[:, :], chosen[:, t, :], start=(t == 0), stop=(t == NT - 1))
                    if b == NT:
                        last.then_inc(counts_ps, 1)
                    for t in range(a, min(b, NT - 1)):
                        left = NT - 1 - t
                        mm(before_bank[:, (t + 1) * E:], ones_bf[:, :],
                           chosen[:, t, :].unsqueeze(1).to_broadcast([P, left, E]), start=(t == 0),
                           stop=False, skip_group_check=True)
                mm(before_bank, strict_bf[:, :], chosen[:, :, :].rearrange("p t e -> p (t e)"),
                   start=False, stop=True, skip_group_check=True).then_inc(before_ps, 1)
                keep_warm(WARM_COUNTS)
                pe.wait_ge(hi_ready, 2 * f + 1)
                keep_warm(WARM_HOTS)
                first_pair = (4 + KT - POOL_Q) * f
                for q in range(KT):
                    if q % (KT // 4) == 0:
                        pe.wait_ge(pair_ready, first_pair + q // (KT // 4) + 1)
                    for k, (a, _) in enumerate(HOTS):
                        if q == a:
                            pe.wait_ge(hot_ready, (len(HOTS) + 1) * f + 1 + k + 1)
                    if q == ACT_Q:
                        pe.wait_ge(act_hot_ready, f + 1)
                    if q >= POOL_Q:
                        pe.wait_ge(pair_ready, first_pair + 4 + q - POOL_Q + 1)
                    last = mm(back_bank, lo_hot[:, q, :], hi_val[:, q, :, :].rearrange("p a s -> p (a s)"),
                              start=(q == 0), stop=(q == KT - 1))
                last.then_inc(back_ps, 1)
                keep_warm(WARM_INVERSE)

            def experts(f):
                base = NS * f
                pe.wait_ge(table_ready, f + 1)
                keep_warm(WARM_EXPERTS)
                pe.wait_ge(expert_w_ready, f + 1)
                if f == 0:
                    pe.wait_ge(w2_in, 16)

                def hidden(j, r, ahead):
                    i = j * RING + r + ahead
                    q = (r + ahead) % RING
                    fills = j + (r + ahead) // RING + 1
                    pe.wait_ge(w1b_in[q], fills * 16 + 16 * (NS // RING) * f)
                    pe.wait_ge(xg_sb, base + i + 1)
                    at_least(pe, h_biased, base + i - RING + 1)
                    for c in range(FC):
                        last = mm(h_bank(q)[:, c * P:(c + 1) * P], w1b[:, q, c * P:(c + 1) * P], xgT[:, q, :],
                                  start=True, stop=True)
                    last.then_inc(h_ps, 1)

                def output(i, r):
                    col = pe.value_load(expert_w[0:1, bass.ds(i, 1)], min_val=0, max_val=(E - 1) * DF)
                    pe.wait_ge(h_gelu, base + i + 1)
                    at_least(pe, y_sb, base + i - RING + 1)
                    for c in range(FC):
                        last = mm(y_bank(r), h_act[:, r, c * P:(c + 1) * P], w2[:, bass.ds(col + c * P, P)],
                                  start=(c == 0), stop=(c == FC - 1))
                    last.then_inc(y_ps, 1)

                def transposed_rows(j, r, ahead):
                    slot_r = (r + ahead) % RING
                    fills = j + (r + ahead) // RING + 1
                    pe.wait_ge(gathered[slot_r], fills * 16 + 16 * (NS // RING) * f)
                    at_least(pe, xg_sb, base + j * RING + r + ahead)
                    pe.transpose(xg_bank, xg[:, slot_r, :], ident[:, :]).then_inc(xg_ps, 1)

                def step(j, r, last=False):
                    i = j * RING + r
                    if not (last and r + 2 >= RING):
                        transposed_rows(j, r, 2)
                    if not (last and r + 1 >= RING):
                        hidden(j, r, 1)
                    if not (isinstance(i, int) and i == 0):
                        output(i - 1, (r - 1) % RING)

                transposed_rows(0, 0, 0)
                hidden(0, 0, 0)
                transposed_rows(0, 1, 0)
                for r in range(RING):
                    step(0, r)
                with pe.Fori(1, NS // RING - 1) as j:
                    for r in range(RING):
                        step(j, r)
                for r in range(RING):
                    step(NS // RING - 1, r, last=True)
                output(NS - 1, (NS - 1) % RING)
                if f == 0:
                    pe.wait_ge(b2_blk_ready, 1)
                pe.wait_ge(w_all_ready, f + 1)
                pe.transpose(w_allT_bank, w_all[:, :, :].rearrange("p t e -> p (t e)"), ident[:, :]).then_inc(w_allT_ps, 1)
                pe.wait_ge(w_allT_sb, f + 1)
                pe.wait_ge(y_sb, NS * (f + 1))
                for c in range(NC):
                    last = mm(banks[:, 2 + c, :], w_allT[:, :],
                              b2_blk[:, c * CH:(c + 1) * CH, :].rearrange("p t n -> p (t n)"), start=True, stop=True)
                    last.then_inc(b2_ps, 1)

            gate()
            route(0)
            experts(0)

            wqkv = w_attn[:, 0:3, :].rearrange("p k n -> p (k n)")

            def turn_3(j, r, bank):
                pe.wait_ge(xn_ready, 2 * j + r + (NT + 1))
                pe.transpose(bank, xn_ring[:, r, :], ident[:, :]).then_inc(xnT_ps, 1)

            def gate_3(j, r, part=0, done=False):
                t = 2 * j + r
                pe.wait_ge(xnT_sb, t + (NC + 1))
                last = mm(logit_bank(1, part)[:, bass.ds(t * E, E)], xnT[:, r * P:(r + 1) * P], wg[:, :],
                          start=True, stop=True)
                if done:
                    last.then_inc(logits_ps, 1)

            def turn_x(i, r):
                pe.wait_ge(xa_sb, i + 1)
                at_least(pe, xaT_sb, i)
                at_least(pe, qT_sb, i - 1)
                pe.transpose(xa_bank, xa[:, r, :], ident[:, :]).then_inc(xa_ps, 1)

            def project(i, r, gate=None):
                at_least(pe, phi_sb, i)
                at_least(pe, exp_sb, i)
                if gate is not None:
                    pe.wait_ge(xnT_sb, 2 * gate + r + NC)
                    turn_3(gate, r, xn_bank)
                mm(qkv_bank, ones2[:, :], bias_2[:, 0:QD], start=True, stop=False)
                pe.wait_ge(xaT_sb, i + 1)
                mm(qkv_bank, xaT[:, r, :], wqkv, start=False, stop=True).then_inc(qkv_ps, 1)

            def turn_m(i, r):
                pe.wait_ge(merged_sb, i + 1)
                at_least(pe, x_attn, i)
                pe.transpose(m_bank, merged[:, r, :], ident[:, :]).then_inc(m_ps, 1)

            def out_proj(i, r):
                pe.wait_ge(mT_sb, i + 1)
                mm(proj_bank, ones2[:, :], bias_2[:, QD:], start=True, stop=False)
                mm(proj_bank, mT[:, r, :], w_attn[:, 3, :], start=False, stop=True).then_inc(proj_ps, 1)

            def attn(j, r, lead=True):
                i = 2 * j + r
                first = isinstance(i, int) and i == 0
                gate = None if isinstance(j, int) and j < 2 else j - 2
                pe.wait_ge(phi_sb, i + 1)
                pe.wait_ge(xaT_sb, i + 2 if lead else NT)
                pe.transpose(qT_bank, qk[:, r, 0:P], ident[:, :]).then_inc(qT_ps, 1)
                pe.wait_ge(kv_sb, i + 1)
                at_least(pe, prod_sb, i)
                n = VE // 3
                for b in range(2):
                    mm(prefix_bank[:, b, :], tri[:, :], kv[:, r, b * n:(b + 1) * n, :].rearrange("p e n -> p (e n)"),
                       start=True, stop=True)
                mm(prefix_bank[:, 2, 0:2 * P], tri[:, :], kv[:, r, 2 * n:, :].rearrange("p e n -> p (e n)"),
                   start=True, stop=True)
                mm(prefix_bank[:, 2, 2 * P:], tri[:, :], qk[:, r, P:2 * P], start=True, stop=True).then_inc(prefix_ps, 1)
                if not first:
                    turn_m(i - 1, 1 - r)
                if lead:
                    turn_x(i + 2, r)
                pe.wait_ge(qT_sb, i + 1)
                if not first:
                    pe.wait_ge(state_sb, i)
                at_least(pe, nd_sb, i)
                if not (isinstance(j, int) and i < 5):
                    gate_3(j - 3 + r, 1 - r)
                mm(inter_bank, qT[:, r, :], state[:, :], start=True, stop=True).then_inc(inter_ps, 1)
                if not first:
                    out_proj(i - 1, 1 - r)
                if lead:
                    project(i + 2, r, gate)
                mm(state_bank, qk[:, r, P:2 * P], vx[:, r, :, :].rearrange("p e h -> p (e h)"),
                   start=first, stop=True, skip_group_check=True).then_inc(state_ps, 1)
                if not lead:
                    pe.wait_ge(phi_sb, NT)
                    pe.wait_ge(exp_sb, NT)
                    pe.wait_ge(xnT_sb, 2 * gate + r + NC)
                    turn_3(gate, r, xn_bank)

            pe.wait_ge(bias_split, 1)
            pe.wait_ge(x_mid, 1)
            keep_warm(WARM_ATTENTION)
            for i in range(2):
                turn_x(i, i)
                project(i, i)
                if i == 0:
                    keep_warm(WARM_PROJECT)
            for j in range(3):
                for r in range(2):
                    attn(j, r)
            with pe.Fori(3, NT // 2 - 1) as j:
                for r in range(2):
                    attn(j, r)
            for r in range(2):
                attn(NT // 2 - 1, r, lead=False)
            pe.wait_ge(nd_sb, NT)
            gate_3((NT - CH) // 2 - 1, 1, done=True)
            turn_3(NT // 2 - 2, 0, xn_tail_bank(0))
            turn_3(NT // 2 - 2, 1, xn_tail_bank(1))
            turn_m(NT - 1, (NT - 1) % 2)
            out_proj(NT - 1, (NT - 1) % 2)
            for r in range(2):
                gate_3(NT // 2 - 2, r, part=1)
            for r in range(2):
                turn_3(NT // 2 - 1, r, xn_tail_bank(2 + r))
                gate_3(NT // 2 - 1, r, part=1, done=(r == 1))
            route(1)
            experts(1)


_INS = ['L0_attn_x', 'L0_attn_Wq', 'L0_attn_bq', 'L0_attn_Wk', 'L0_attn_bk', 'L0_attn_Wv', 'L0_attn_bv',
        'L0_attn_Wo', 'L0_attn_bo', 'L0_ffn_Wg', 'W1b', 'L0_ffn_W2', 'L0_ffn_b2']


def kernel(**inputs):
    import numpy as _np
    import concourse.bacc as _bacc
    from concourse import mybir as _mybir
    from concourse.bass_utils import run_bass_kernel_spmd as _run

    nc = _bacc.Bacc("TRN2", target_bir_lowering=False, num_devices=1)
    W1, b1 = _np.asarray(inputs['L0_ffn_W1']), _np.asarray(inputs['L0_ffn_b1'])
    E, D, DF = W1.shape
    inputs['W1b'] = _np.concatenate([W1, b1.reshape(E, DF // P, P).transpose(0, 2, 1)], axis=2)
    arrays, args = {}, []
    for name in _INS:
        a = _np.ascontiguousarray(inputs[name])
        arrays[f"in_{name}"] = a
        args.append(nc.dram_tensor(f"in_{name}", a.shape, _mybir.dt.from_np(a.dtype), kind="ExternalInput").ap())
    shape = inputs['L0_attn_x'].shape
    out = nc.dram_tensor("out_0", shape, _mybir.dt.float32, kind="ExternalOutput").ap()
    macaron_kernel(nc, *args, out)
    r = _run(nc, [arrays], core_ids=[0])
    return r.results[0]["out_0"]
```
